# Optimizing a Trainium2 kernel written in Bass

```python
import numpy as np
import jax
import jax.numpy as jnp

def _softmax(x, axis=-1):
    return jax.nn.softmax(x, axis=axis)

def _gelu(x):
    return jax.nn.gelu(x, approximate=True)

def _silu(x):
    return jax.nn.silu(x)

def _sigmoid(x):
    return jax.nn.sigmoid(x)

def _layernorm(x, axis=-1, eps=1e-05):
    m = jnp.mean(x, axis=axis, keepdims=True)
    v = jnp.var(x, axis=axis, keepdims=True)
    return (x - m) / jnp.sqrt(v + eps)

def _scatter_add(tgt, idx, src, axis=0):
    return tgt.at[idx].add(src)

def _segment_sum(src, seg, n):
    return jax.ops.segment_sum(src, seg, n)
kernel_name = 'mk_adj_resnorm_d2_adj_r2_d5391d'

def setup_inputs(seed: int=0):
    np.random.seed(seed)
    _w = jnp.asarray

    def _rec_inputs():
        import jax
        import jax.numpy as jnp
        _gk = jax.random.key(seed)
        x = 7.22e-05 + 1 * jax.random.normal(jax.random.fold_in(_gk, 1), (16, 512, 256), jnp.float32)
        _w = (1.0 + jnp.arange(512, dtype=jnp.float32)) ** (-0.5)
        _w = _w / _w.mean()
        _pij = jnp.clip(0.03125 * _w[:, None] * _w[None, :], 0.0, 1.0)
        _a = jax.random.uniform(jax.random.fold_in(_gk, 2), (16, 512, 512)) < _pij
        adj = _a.astype(jnp.int32)
        return (x, adj)
    x, adj = _rec_inputs()

    def _L0_gnn_setup():
        import jax, jax.numpy as jnp
        import numpy as np
        ALPHA = 0.2
        NEG_INF = -1000000000.0
        key = jax.random.key(seed)
        k1, k2, k3, k4 = jax.random.split(key, 4)
        B, N, IN, OUT = (8, 1024, 256, 32)
        graph_input = jax.random.normal(k1, (B, N, IN), dtype=jnp.float32)
        adj = jax.random.randint(k2, (B, N, N), 0, 2, dtype=jnp.int32)
        W_fc = jax.random.normal(k3, (OUT, IN), dtype=jnp.float32) * (1.0 / np.sqrt(IN))
        W_attn = jax.random.normal(k4, (1, 2 * OUT), dtype=jnp.float32) * (1.0 / np.sqrt(2 * OUT))
        return {'graph_input': graph_input, 'adj': adj, 'W_fc': W_fc, 'W_attn': W_attn}
    _L0_gnn_all = _L0_gnn_setup()
    _L0_gnn_in = {k: v for k, v in _L0_gnn_all.items() if k in ('W_fc', 'W_attn')}
    del _L0_gnn_all

    def _L1_gnn_setup():
        import jax, jax.numpy as jnp
        import numpy as np
        B, N, H, NH = (8, 512, 256, 8)
        DK = H // NH
        key = jax.random.key(seed)
        ks = jax.random.split(key, 6)
        x = jax.random.normal(ks[0], (B, N, H), dtype=jnp.float32)
        adj = jax.random.randint(ks[1], (B, N, N), 0, 2, dtype=jnp.int32)
        adj = jnp.maximum(adj, jnp.eye(N, dtype=jnp.int32)[None])
        s = 1.0 / np.sqrt(H)
        Wq = jax.random.normal(ks[2], (H, H), dtype=jnp.float32) * s
        Wk = jax.random.normal(ks[3], (H, H), dtype=jnp.float32) * s
        Wv = jax.random.normal(ks[4], (H, H), dtype=jnp.float32) * s
        Wg = jax.random.normal(ks[5], (H, 2 * H), dtype=jnp.float32) * (1.0 / np.sqrt(2 * H))
        bg = jnp.zeros((H,), dtype=jnp.float32)
        return {'x': x, 'adj': adj, 'Wq': Wq, 'Wk': Wk, 'Wv': Wv, 'Wg': Wg, 'bg': bg}
    _L1_gnn_all = _L1_gnn_setup()
    _L1_gnn_in = {k: v for k, v in _L1_gnn_all.items() if k in ('Wq', 'Wk', 'Wv', 'Wg', 'bg')}
    del _L1_gnn_all
    return {'x': x, 'adj': adj, 'L0_gnn_W_fc': _L0_gnn_in['W_fc'], 'L0_gnn_W_attn': _L0_gnn_in['W_attn'], 'L1_gnn_Wq': _L1_gnn_in['Wq'], 'L1_gnn_Wk': _L1_gnn_in['Wk'], 'L1_gnn_Wv': _L1_gnn_in['Wv'], 'L1_gnn_Wg': _L1_gnn_in['Wg'], 'L1_gnn_bg': _L1_gnn_in['bg']}

def reference(x, adj, L0_gnn_W_fc, L0_gnn_W_attn, L1_gnn_Wq, L1_gnn_Wk, L1_gnn_Wv, L1_gnn_Wg, L1_gnn_bg):
    import jax
    import jax.numpy as jnp

    def _L0_gnn_ref(graph_input, adj, W_fc, W_attn):
        import jax, jax.numpy as jnp
        import numpy as np
        ALPHA = 0.2
        NEG_INF = -1000000000.0
        h = jnp.einsum('bni,oi->bno', graph_input, W_fc)
        out_dim = W_fc.shape[0]
        a1 = W_attn[0, :out_dim]
        a2 = W_attn[0, out_dim:]
        f1 = jnp.einsum('bno,o->bn', h, a1)
        f2 = jnp.einsum('bno,o->bn', h, a2)
        scores = jax.nn.leaky_relu(f1[:, :, None] + f2[:, None, :], negative_slope=ALPHA)
        scores = jnp.where(adj == 0, NEG_INF, scores)
        attn = jax.nn.softmax(scores, axis=2)
        h_prime = jnp.einsum('bnm,bmi->bni', attn, graph_input)
        return jax.nn.elu(h_prime)

    def _L1_gnn_ref(x, adj, Wq, Wk, Wv, Wg, bg):
        import jax, jax.numpy as jnp
        import numpy as np
        B, N, H, NH = (8, 512, 256, 8)
        DK = H // NH
        b, n, h = x.shape
        q = (x @ Wq.T).reshape(b, n, NH, DK)
        k = (x @ Wk.T).reshape(b, n, NH, DK)
        v = (x @ Wv.T).reshape(b, n, NH, DK)
        scores = jnp.einsum('bqhd,bkhd->bhqk', q, k) / jnp.sqrt(jnp.float32(DK))
        mask = (adj != 0)[:, None, :, :]
        scores = jnp.where(mask, scores, -jnp.inf)
        attn = jax.nn.softmax(scores, axis=-1)
        c = jnp.einsum('bhqk,bkhd->bqhd', attn, v).reshape(b, n, h)
        gate = jax.nn.sigmoid(jnp.concatenate([c, x], axis=2) @ Wg.T + bg)
        return gate * x + (1.0 - gate) * c
    x = _layernorm(x + _L0_gnn_ref(x, adj, L0_gnn_W_fc, L0_gnn_W_attn), axis=-1)
    x = _layernorm(x + _L1_gnn_ref(x, adj, L1_gnn_Wq, L1_gnn_Wk, L1_gnn_Wv, L1_gnn_Wg, L1_gnn_bg), axis=-1)
    return x

_drawn_inputs = setup_inputs


def setup_inputs(seed=0):
    import zlib

    import numpy as np

    out = dict(_drawn_inputs(seed))
    spreads = {'L1_gnn_bg': (0.0, 0.49)}
    factors = {}
    for name, (base, spread) in spreads.items():
        noise = np.random.default_rng([zlib.crc32(name.encode()), seed]).standard_normal(out[name].shape)
        drawn = base * np.exp(spread * noise) if base else spread * noise
        out[name] = jnp.asarray(drawn.astype(out[name].dtype))
    for name, factor in factors.items():
        out[name] = (out[name] * factor).astype(out[name].dtype)
    return out
```

```python
from contextlib import ExitStack

import concourse.bass as bass
from concourse import mybir

ALU = mybir.AluOpType
ACT = mybir.ActivationFunctionType
F32 = mybir.dt.float32
F32R = mybir.dt.float32r
BF16 = mybir.dt.bfloat16
I32 = mybir.dt.int32

P = 128
NH = 8
MASKED = -1e30
EPS = 1e-5
SLOPE = 0.2
BIG = 3e38


def two_layer_gat(nc, x, adj, w_fc, w_attn, wq_t, wk_t, wv_t, wg_t, bg, eye, out):
    B, N, H = x.shape
    NT = N // P
    KT = H // P
    DK = H // NH
    HPH = P // DK
    OF = w_fc.shape[0]
    SCALE = float(DK) ** -0.5
    U = NH * NT
    Q = U // 4
    PARTS = P // DK
    PACK = 16 * 2 * PARTS
    assert (N, H, NT, KT, DK, HPH, U, B % 2) == (512, 256, 4, 2, 32, 4, 32, 0)

    def unit(u):
        qq, j, r = u // Q, u % Q // 2, u % 2
        return qq, j, r, qq // 2 * HPH + j, qq % 2 * 2 + r

    def by_vector(u):
        return u % 4 == 3

    def vector_copies(u):
        return (u + 1) // 4

    def scalar_copies(u):
        return u + 1 - vector_copies(u)

    def wait(eng, sem, value):
        if not (isinstance(value, int) and value <= 0):
            eng.wait_ge(sem, value)

    def hold(eng):
        eng.nop(nofuse=True)

    with ExitStack() as ctx:
        def sb(name, shape, dt=F32):
            return ctx.enter_context(nc.sbuf_tensor(name, shape, dt))

        def sem(name):
            return ctx.enter_context(nc.semaphore(name))

        x_in = sb("x_in", [P, 2, NT, H])
        adj_in = sb("adj_in", [P, NT, N], I32)
        mask_add = sb("mask_add", [P, 2, NT, N], BF16)
        z = sb("z", [P, NT, N])
        z_t = sb("z_t", [P, NT, N])
        hx = sb("hx", [P, NT, H])
        ey = sb("ey", [P, NT, H])
        x1_t = sb("x1_t", [P, 2, KT, N])
        x1_hi = sb("x1_hi", [P, 2, KT, N], F32R)
        x1_lo = sb("x1_lo", [P, 2, KT, N], F32R)
        stage = sb("stage", [P, 4, 2, N], F32R)
        q_pack = sb("q_pack", [P, NH, N], F32R)
        k_pack = sb("k_pack", [P, NH, N], F32R)
        v = sb("v", [P, NT, H])
        probs = sb("probs", [P, 2, N])
        probs_t = sb("probs_t", [P, 2, HPH, NT, 2 * P])
        recip_b = sb("recip_b", [P, N])
        c_t = sb("c_t", [P, 2, N])
        th = sb("th", [P, KT, N])
        diff = sb("diff", [P, KT, N])
        summ = sb("summ", [P, KT, N])
        y_out = sb("y_out", [P, NT, H])
        w_hi = sb("w_hi", [P, 4, KT, H], F32R)
        w_lo = sb("w_lo", [P, 4, KT, H], F32R)
        w_gc = sb("w_gc", [P, KT, H])
        wf = sb("wf", [P, 2, H])
        ident = sb("ident", [P, P])
        fc_in = y_out[0:OF, 0]
        attn_in = sb("attn_in", [OF, 2])
        gate_b = sb("gate_b", [P, KT])
        half_b = sb("half_b", [P, KT])
        f12 = sb("f12", [P, 2, 2, NT])
        z_max = sb("z_max", [P, NT])
        z_nmf = sb("z_nmf", [P, NT])
        z_bias = sb("z_bias", [P, NT])
        z_sum = sb("z_sum", [P, NT])
        z_rec = sb("z_rec", [P, NT])
        valid = sb("valid", [P, 2, NT])
        s_min = sb("s_min", [P, U])
        s_sum = sb("s_sum", [P, NH, NT])
        s_val = sb("s_val", [P, NH, NT])
        s_rec = sb("s_rec", [P, NH, NT])
        s_wide = sb("s_wide", [P, NT, HPH, DK])
        stats = sb("stats", [P, 2, NT, 6])
        mean_var = sb("mean_var", [P, 2, NT, 2])
        var_eps = sb("var_eps", [P, 2, NT])
        rstd = sb("rstd", [P, 2, NT])
        neg_mean = sb("neg_mean", [P, NT])
        neg_half = sb("neg_half", [P, NT])

        ps_s = [ctx.enter_context(nc.psum_tensor(f"ps_s{k}", [P, N], F32)) for k in range(2)]
        ps_t = [ctx.enter_context(nc.psum_tensor(f"ps_t{k}", [P, N], F32)) for k in range(2)]
        ps_c = ctx.enter_context(nc.psum_tensor("ps_c", [P, N], F32))
        misc = [ctx.enter_context(nc.psum_tensor(f"misc{k}", [P, N], F32)) for k in range(3)]

        weights_in = sem("weights_in")
        consts_in = sem("consts_in")
        w_hi_done = sem("w_hi_done")
        w_lo_done = sem("w_lo_done")
        wf_mm = sem("wf_mm")
        wf_done = sem("wf_done")
        half_done = sem("half_done")
        x_loaded = sem("x_loaded")
        adj_loaded = sem("adj_loaded")
        packed = [sem(f"packed{h}") for h in range(NH)]
        stored = sem("stored")
        f_done = sem("f_done")
        mask_done = sem("mask_done")
        f2_rows = sem("f2_rows")
        z_masked = sem("z_masked")
        z_added = sem("z_added")
        z_leaky = sem("z_leaky")
        z_nmf_done = sem("z_nmf_done")
        z_bias_done = sem("z_bias_done")
        z_exp = sem("z_exp")
        z_turned = sem("z_turned")
        z_copied = sem("z_copied")
        z_rec_done = sem("z_rec_done")
        agg_done = sem("agg_done")
        h_done = sem("h_done")
        e_done = sem("e_done")
        res_done = sem("res_done")
        y1_done = sem("y1_done")
        stats1 = sem("stats1")
        aggr1 = sem("aggr1")
        rstd1 = sem("rstd1")
        x1_done = sem("x1_done")
        x1_turned = sem("x1_turned")
        x1_copied = sem("x1_copied")
        x1_hi_done = sem("x1_hi_done")
        x1_lo_done = sem("x1_lo_done")
        qk_mm = sem("qk_mm")
        qk_hi = sem("qk_hi")
        qk_lo = sem("qk_lo")
        v_mm = sem("v_mm")
        v_done = sem("v_done")
        s_mm = sem("s_mm")
        s_masked = sem("s_masked")
        s_exp = sem("s_exp")
        p_turned = sem("p_turned")
        p_scalar = sem("p_scalar")
        p_vector = sem("p_vector")
        c_mm = sem("c_mm")
        sum_valid = sem("sum_valid")
        rec_done = sem("rec_done")
        rec_wide = sem("rec_wide")
        rec_rows = sem("rec_rows")
        rec_copied = sem("rec_copied")
        c_done = sem("c_done")
        gate_mm = sem("gate_mm")
        tanh_done = sem("tanh_done")
        ds_done = sem("ds_done")
        u_done = sem("u_done")
        y2_done = sem("y2_done")
        y_turned = sem("y_turned")
        stats2 = sem("stats2")
        aggr2 = sem("aggr2")
        rstd2 = sem("rstd2")
        applied = sem("applied")

        block = ctx.enter_context(nc.Block())

        def run(eng, step):
            step(-1, attend=False, pre=True, post=False, ahead=True)
            step(0, attend=True, pre=True, post=False, ahead=True)
            with eng.Fori(0, (B - 4) // 2) as i:
                step(2 * i + 1, attend=True, pre=True, post=True, ahead=True, parity=1)
                step(2 * i + 2, attend=True, pre=True, post=True, ahead=True, parity=0)
            step(B - 3, attend=True, pre=True, post=True, ahead=True)
            step(B - 2, attend=True, pre=True, post=True, ahead=False)
            step(B - 1, attend=True, pre=False, post=True, ahead=False)
            step(B, attend=False, pre=False, post=True, ahead=False)

        @block.sync
        def _(sp):
            sp.dma_start(ident[:], eye).then_inc(consts_in, 16)
            sp.dma_start(fc_in, w_fc).then_inc(consts_in, 16)
            sp.dma_start(attn_in[:], w_attn).then_inc(consts_in, 16)
            sp.dma_start(gate_b[:], bg).then_inc(consts_in, 16)

            def load_x(g, par):
                src = x[bass.ds(g, 1)].rearrange("g (t p) i -> p (g t) i", p=P)
                sp.dma_start(x_in[:, par], src).then_inc(x_loaded, 16)

            def load_adj(g):
                src = adj[bass.ds(g, 1)].rearrange("g (t p) m -> p (g t) m", p=P)
                sp.dma_start(adj_in[:], src).then_inc(adj_loaded, 16)

            load_x(0, 0)
            load_adj(0)
            raw = probs_t[:].rearrange("p a h k q -> p (a h k) q")
            for n, w in enumerate((wq_t, wk_t, wv_t)):
                sp.dma_start(raw[:, KT * n:KT * n + KT], w.rearrange("(t p) o -> p t o", p=P)).then_inc(weights_in, 16)
            sp.dma_start(raw[:, 3 * KT:4 * KT], wg_t[H:2 * H].rearrange("(t p) o -> p t o", p=P)).then_inc(weights_in, 16)
            sp.dma_start(w_gc[:], wg_t[0:H].rearrange("(t p) o -> p t o", p=P)).then_inc(weights_in, 16)

            def pack_head(half, j):
                h = half * HPH + j
                rows = slice(j * DK, j * DK + DK)
                for dst, n, order in ((q_pack, 2 * half, (0, 0, 1, 1)), (k_pack, 2 * half + 1, (0, 1, 0, 1))):
                    for part, lo in enumerate(order):
                        sp.dma_start(dst[part * DK:part * DK + DK, h].bitcast(F32),
                                     stage[rows, n, lo].bitcast(F32)).then_inc(packed[h], 16)

            def step(b, attend, pre, post, ahead, parity=None):
                par = b % 2 if parity is None else parity
                if ahead:
                    wait(sp, res_done, b + 1)
                    hold(sp)
                    load_x(b + 2, par)
                if attend:
                    for j in range(HPH):
                        if j == 0:
                            sp.wait_ge(qk_lo, 4 * b + 4)
                            hold(sp)
                        wait(sp, s_mm, U * (b - 1) + 3 * Q + 2 * j + 2)
                        pack_head(1, j)
                if ahead:
                    wait(sp, mask_done, b + 2)
                    hold(sp)
                    load_adj(b + 2)
                if pre:
                    for j in range(HPH):
                        if j == 0:
                            sp.wait_ge(qk_lo, 4 * (b + 1) + 2)
                            hold(sp)
                        wait(sp, s_mm, U * b + Q + 2 * j + 2)
                        pack_head(0, j)
                if post:
                    sp.wait_ge(applied, NT * b)
                    hold(sp)
                    dst = out[bass.ds(b - 1, 1)].rearrange("g (t p) i -> p (g t) i", p=P)
                    sp.dma_start(dst, y_out[:]).then_inc(stored, 16)

            run(sp, step)
            sp.wait_ge(stored, 16 * B)

        @block.tensor
        def _(pe):
            mm = nc.tensor.matmul

            pe.wait_ge(consts_in, 64)
            for a in range(2):
                last = mm(misc[0][:, a * H:a * H + H], attn_in[:, a:a + 1].to_broadcast([OF, P]), fc_in,
                          start=True, stop=True)
            last.then_inc(wf_mm, 1)

            def scores(b, u):
                qq, j, r, h, qt = unit(u)
                if qq % 2 == 0 and r == 0:
                    pe.wait_ge(packed[h], PACK * (b + 1))
                wait(pe, s_exp, U * b + u - 1)
                mm(ps_s[u % 2][:], q_pack[:, h, qt * P:qt * P + P], k_pack[:, h],
                   start=True, stop=True).then_inc(s_mm, 1)

            def turn(b, u):
                if u >= 2:
                    if by_vector(u - 2):
                        wait(pe, p_vector, U // 4 * b + vector_copies(u - 2))
                    else:
                        wait(pe, p_scalar, 3 * U // 4 * b + scalar_copies(u - 2))
                else:
                    if by_vector(u - 2 + U):
                        wait(pe, p_vector, U // 4 * (b - 1) + vector_copies(u - 2 + U))
                    else:
                        wait(pe, p_scalar, 3 * U // 4 * (b - 1) + scalar_copies(u - 2 + U))
                pe.wait_ge(s_exp, U * b + u + 1)
                for kt in range(NT):
                    last = nc.tensor.transpose(ps_t[u % 2][:, kt * P:kt * P + P],
                                               probs[:, u % 2, kt * P:kt * P + P], ident[:])
                last.then_inc(p_turned, 1)

            def attend_v(b, qq, kt):
                half, qh = qq // 2, qq % 2
                if kt == 0:
                    u = qq * Q + Q - 1
                    pe.wait_ge(p_vector, U // 4 * b + vector_copies(u))
                    pe.wait_ge(p_scalar, 3 * U // 4 * b + scalar_copies(u))
                    if qq == 0:
                        pe.wait_ge(v_done, 2 * b + 2)
                    if qh == 0:
                        wait(pe, c_done, 2 * b + half)
                for j in range(HPH):
                    h = half * HPH + j
                    last = mm(ps_c[j * DK:j * DK + DK, qh * 2 * P:qh * 2 * P + 2 * P], v[:, kt, h * DK:h * DK + DK],
                              probs_t[:, qq % 2, j, kt], start=(kt == 0), stop=(kt == NT - 1))
                if kt == NT - 1:
                    last.then_inc(c_mm, 1)

            def recip_rows(b, half, bank):
                pe.wait_ge(rec_wide, 2 * b + half + 1)
                for qt in range(NT):
                    last = nc.tensor.transpose(bank[:, qt * P:qt * P + P], s_wide[:, qt].rearrange("p j d -> p (j d)"),
                                               ident[:])
                last.then_inc(rec_rows, 1)

            def split_mm(dst, pairs):
                for n, (a, c) in enumerate(pairs):
                    last = mm(dst, a, c, start=(n == 0), stop=(n == len(pairs) - 1))
                return last

            def step(b, attend, pre, post, ahead, parity=None):
                par = b % 2 if parity is None else parity
                nxt, prv = 1 - par, 1 - par
                p, q = b + 1, b - 1
                for u in range(U):
                    if attend:
                        scores(b, u)
                    if u >= 2 and attend:
                        turn(b, u - 2)
                    if u < 2 and post:
                        turn(q, u - 2 + U)
                    if u >= 14 and u % 8 >= 6 and attend:
                        attend_v(b, (u - 14) // 8, u % 8 - 6)
                    if u >= 16 and u % 8 < 2 and attend:
                        attend_v(b, (u - 14) // 8, u % 8 + 2)
                    if u < 2 and post:
                        attend_v(q, 2, u + 2)
                    if 6 <= u < 10 and post:
                        attend_v(q, 3, u - 6)

                    if u == 0 and pre:
                        wait(pe, applied, NT * q)
                        wait(pe, qk_lo, 4 * p - 1)
                        if isinstance(p, int) and p == 0:
                            pe.wait_ge(wf_done, 1)
                        pe.wait_ge(f_done, 2 * NT * p + 2 * NT)
                        for t in range(NT):
                            last = nc.tensor.transpose(misc[0][:, t * P:t * P + P],
                                                       f12[:, nxt, 1, t:t + 1].to_broadcast([P, P]), ident[:])
                        last.then_inc(f2_rows, 1)
                    if u == 4 and post:
                        wait(pe, applied, NT * q)
                        wait(pe, rec_copied, 2 * q + 1)
                        recip_rows(q, 1, misc[1])
                    if 8 <= u < 12 and pre:
                        t = u - 8
                        if t == 0:
                            wait(pe, qk_lo, 4 * p)
                        if t == 1 and post:
                            pe.wait_ge(rec_copied, 2 * b)
                        if t >= 2:
                            pe.wait_ge(z_copied, NT * p + t - 1)
                        pe.wait_ge(z_exp, NT * p + t + 1)
                        bank = misc[2 - t % 2]
                        for mt in range(NT):
                            last = nc.tensor.transpose(bank[:, mt * P:mt * P + P], z[:, t, mt * P:mt * P + P], ident[:])
                        last.then_inc(z_turned, 1)
                    if u in (9, 11) and attend:
                        n = (u - 9) // 2
                        if n == 0 and pre:
                            pe.wait_ge(z_masked, NT * p + NT)
                        if n == 0 and not pre:
                            pe.wait_ge(applied, NT * q)
                        if n == 1:
                            pe.wait_ge(v_done, 2 * b + 1)
                        if n == 0:
                            pe.wait_ge(x1_lo_done, b + 1)
                        for s in range(2):
                            t = 2 * n + s
                            rows = slice(t * P, t * P + P)
                            pairs = [(a[:, par, kt, rows], w[:, 2, kt]) for kt in range(KT)
                                     for a, w in ((x1_hi, w_hi), (x1_hi, w_lo), (x1_lo, w_hi))]
                            last = split_mm(misc[0][:, s * H:s * H + H], pairs)
                        last.then_inc(v_mm, 1)
                    if 12 <= u < 16 and pre:
                        t = u - 12
                        if t == 0:
                            pe.wait_ge(z_copied, NT * p + 3)
                        if t == 2:
                            pe.wait_ge(z_copied, NT * p + 4)
                        bank = misc[2 - t // 2]
                        for mt in range(NT):
                            last = mm(bank[:, t % 2 * H:t % 2 * H + H], z_t[:, mt, t * P:t * P + P], x_in[:, nxt, mt],
                                      start=(mt == 0), stop=(mt == NT - 1))
                        if t % 2 == 1:
                            last.then_inc(agg_done, 1)
                    if u in (17, 19) and post:
                        oh = (u - 17) // 2
                        if oh == 0:
                            if attend:
                                pe.wait_ge(v_done, 2 * b + 2)
                            else:
                                pe.wait_ge(applied, NT * q)
                            pe.wait_ge(c_done, 2 * b)
                        elif pre:
                            pe.wait_ge(h_done, NT * p + 2)
                        cols = slice(oh * P, oh * P + P)
                        pairs = [(w[:, 3, kt, cols], a[:, prv, kt]) for kt in range(KT)
                                 for w, a in ((w_hi, x1_hi), (w_lo, x1_hi), (w_hi, x1_lo))]
                        pairs += [(w_gc[:, kt, cols], c_t[:, kt]) for kt in range(KT)]
                        split_mm(misc[2 * oh][:], pairs).then_inc(gate_mm, 1)
                    if u == 22 and pre:
                        for kt in range(KT):
                            if kt == 0:
                                pe.wait_ge(h_done, NT * p + NT)
                                pe.wait_ge(x1_done, NT * p + NT)
                            elif post:
                                pe.wait_ge(tanh_done, 2 * q + 1)
                            elif attend:
                                pe.wait_ge(v_done, 2 * b + 2)
                            for t in range(NT):
                                last = nc.tensor.transpose(misc[1 - kt][:, t * P:t * P + P],
                                                           hx[:, t, kt * P:kt * P + P], ident[:])
                            last.then_inc(x1_turned, 1)
                    if u == 27 and attend:
                        if pre:
                            pe.wait_ge(qk_lo, 4 * p + 2)
                        else:
                            pe.wait_ge(rec_copied, 2 * b)
                        recip_rows(b, 0, misc[1])
                    if 24 <= u < 28 and pre:
                        n = u - 24
                        if n == 0:
                            pe.wait_ge(x1_lo_done, p + 1)
                            if post:
                                pe.wait_ge(tanh_done, 2 * q + 2)
                        if n == 3:
                            pe.wait_ge(qk_lo, 4 * p + 1)
                        cols = slice(n // 2 * P, n // 2 * P + P)
                        w0 = n % 2
                        pairs = [(w[:, w0, kt, cols], a[:, nxt, kt]) for kt in range(KT)
                                 for w, a in ((w_hi, x1_hi), (w_lo, x1_hi), (w_hi, x1_lo))]
                        split_mm(misc[(2, 1, 0, 2)[n]][:], pairs).then_inc(qk_mm, 1)
                    if u in (28, 29) and post:
                        n = u - 28
                        if n == 0:
                            pe.wait_ge(y2_done, b)
                            if pre:
                                pe.wait_ge(qk_lo, 4 * p + 3)
                            else:
                                pe.wait_ge(tanh_done, 2 * q + 1)
                        elif attend:
                            pe.wait_ge(rec_copied, 2 * b + 1)
                        for t in (2 * n, 2 * n + 1):
                            for kt in range(KT):
                                last = nc.tensor.transpose(
                                    misc[n][:, t % 2 * H + kt * P:t % 2 * H + kt * P + P],
                                    summ[:, kt, t * P:t * P + P], ident[:])
                        last.then_inc(y_turned, 1)

            pe.wait_ge(w_lo_done, 4)
            run(pe, step)

        @block.vector
        def _(dve):
            vec = nc.vector
            raw = probs_t[:].rearrange("p a h k q -> p (a h k) q")
            vec.memset(neg_half[:], -0.5).then_inc(half_done, 1)
            dve.wait_ge(consts_in, 64)
            vec.tensor_scalar(half_b[:], gate_b[:], 0.5, None, ALU.mult).then_inc(half_done, 1)
            dve.wait_ge(wf_mm, 1)
            vec.tensor_copy(wf[:], misc[0][:].rearrange("p (a i) -> p a i", a=2)).then_inc(wf_done, 1)
            dve.wait_ge(wf_done, 1)
            dve.wait_ge(weights_in, 80)
            for n in range(4):
                vec.tensor_copy(w_hi[:, n], raw[:, KT * n:KT * n + KT]).then_inc(w_hi_done, 1)
                dve.wait_ge(w_hi_done, n + 1)
                vec.tensor_tensor(w_lo[:, n], raw[:, KT * n:KT * n + KT], w_hi[:, n].bitcast(F32),
                                  ALU.subtract).then_inc(w_lo_done, 1)
            dve.wait_ge(w_lo_done, 4)

            def node_terms(g, par, t):
                if t == 0:
                    dve.wait_ge(x_loaded, 16 * g + 16)
                for a in range(2):
                    wait(dve, f_done, 2 * NT * g + 2 * t + a - 1)
                    vec.tensor_tensor_reduce(y_out[:, (2 * t + a) % 2], x_in[:, par, t], wf[:, a], 1.0, 0.0,
                                             ALU.mult, ALU.add, f12[:, par, a, t:t + 1]).then_inc(f_done, 1)

            def copy_turned(b, u):
                qq, j, r, h, qt = unit(u)
                dve.wait_ge(p_turned, U * b + u + 1)
                wait(dve, c_mm, 4 * b + qq - 1)
                vec.tensor_copy(probs_t[:, qq % 2, j, :, r * P:r * P + P],
                                ps_t[u % 2][:].rearrange("p (k q) -> p k q", k=NT)).then_inc(p_vector, 1)

            def recip(b, half, par):
                hs = slice(half * HPH, half * HPH + HPH)
                dve.wait_ge(s_exp, U * b + U // 2 * (half + 1))
                vec.tensor_tensor(s_val[:, hs], s_sum[:, hs],
                                  valid[:, par].unsqueeze(1).to_broadcast([P, HPH, NT]), ALU.mult).then_inc(sum_valid, 1)
                dve.wait_ge(sum_valid, 2 * b + half + 1)
                vec.reciprocal(s_rec[:, hs], s_val[:, hs]).then_inc(rec_done, 1)
                dve.wait_ge(rec_done, 2 * b + half + 1)
                wait(dve, rec_rows, 2 * b + half)
                vec.tensor_copy(s_wide[:], s_rec[:, hs].rearrange("p j t -> p t j").unsqueeze(3)
                                .to_broadcast([P, NT, HPH, DK])).then_inc(rec_wide, 1)

            def normalise(b, half):
                dve.wait_ge(c_mm, 4 * b + 2 * half + 2)
                dve.wait_ge(rec_copied, 2 * b + half + 1)
                wait(dve, gate_mm, 2 * b)
                wait(dve, ds_done, 2 * b)
                vec.tensor_tensor(c_t[:, half], ps_c[:], recip_b[:], ALU.mult).then_inc(c_done, 1)

            def step(b, attend, pre, post, ahead, parity=None):
                par = b % 2 if parity is None else parity
                nxt, prv = 1 - par, 1 - par
                p, q = b + 1, b - 1
                if isinstance(b, int) and b == -1:
                    for t in range(NT):
                        node_terms(0, 0, t)
                for u in range(U):
                    if attend:
                        qt = unit(u)[4]
                        dve.wait_ge(s_mm, U * b + u + 1)
                        hold(dve)
                        vec.tensor_tensor_reduce(ps_s[u % 2][:], ps_s[u % 2][:], mask_add[:, par, qt], -SCALE, BIG,
                                                 ALU.add, ALU.min, s_min[:, u:u + 1]).then_inc(s_masked, 1)
                    if u >= 3 and by_vector(u - 3) and attend:
                        copy_turned(b, u - 3)
                    if u < 3 and by_vector(u - 3 + U) and post:
                        copy_turned(q, u - 3 + U)

                    if u == 1 and pre:
                        dve.wait_ge(adj_loaded, 16 * p + 16)
                        vec.tensor_scalar(mask_add[:, nxt], adj_in[:], 0.0, MASKED,
                                          ALU.is_equal, ALU.mult).then_inc(mask_done, 1)
                    if 2 <= u < 6 and pre:
                        t = u - 2
                        if t == 0:
                            wait(dve, z_turned, NT * p)
                            dve.wait_ge(f2_rows, p + 1)
                        dve.wait_ge(mask_done, p + 1)
                        hold(dve)
                        vec.tensor_tensor_reduce(z[:, t], misc[0][:], mask_add[:, nxt, t], 1.0, -BIG,
                                                 ALU.add, ALU.max, z_max[:, t:t + 1]).then_inc(z_masked, 1)
                    if u == 2 and post:
                        recip(q, 1, prv)
                    if u == 5 and pre:
                        dve.wait_ge(z_masked, NT * p + NT)
                        vec.scalar_tensor_tensor(z_nmf[:], z_max[:], -1.0, f12[:, nxt, 0], ALU.mult,
                                                 ALU.subtract).then_inc(z_nmf_done, 1)
                        vec.tensor_scalar(valid[:, nxt], z_max[:], MASKED / 10, None, ALU.is_gt).then_inc(z_nmf_done, 1)
                        dve.wait_ge(z_nmf_done, 2 * p + 2)
                        vec.scalar_tensor_tensor(z_bias[:], z_nmf[:], SLOPE, z_nmf[:], ALU.mult,
                                                 ALU.min).then_inc(z_bias_done, 1)
                    if 4 <= u < 8 and pre:
                        t = u - 4
                        dve.wait_ge(z_added, NT * p + t + 1)
                        vec.scalar_tensor_tensor(z[:, t], z[:, t], SLOPE, z[:, t], ALU.mult,
                                                 ALU.max).then_inc(z_leaky, 1)
                    if u == 10 and pre:
                        dve.wait_ge(z_exp, NT * p + NT)
                        vec.reciprocal(z_rec[:], z_sum[:]).then_inc(z_rec_done, 1)
                    if u == 11 and post:
                        normalise(q, 1)
                    if u == 17 and pre:
                        dve.wait_ge(e_done, p + 1)
                        dve.wait_ge(h_done, NT * p + NT)
                        vec.scalar_tensor_tensor(hx[:], hx[:], 0.0, x_in[:, nxt], ALU.max, ALU.add).then_inc(res_done, 1)
                        dve.wait_ge(res_done, p + 1)
                        vec.scalar_tensor_tensor(ey[:], ey[:], 1.0, hx[:], ALU.min, ALU.add).then_inc(y1_done, 1)
                    if u == 18 and pre:
                        dve.wait_ge(y1_done, p + 1)
                        for t in range(NT):
                            vec.bn_stats(stats[:, 0, t], ey[:, t]).then_inc(stats1, 1)
                        wait(dve, x1_done, NT * p)
                        for t in range(NT):
                            dve.wait_ge(stats1, NT * p + t + 1)
                            hold(dve)
                            vec.bn_aggr(mean_var[:, 0, t], stats[:, 0, t]).then_inc(aggr1, 1)
                    if u == 21 and post:
                        dve.wait_ge(tanh_done, 2 * q + 2)
                        dve.wait_ge(ds_done, 2 * q + 2)
                        vec.scalar_tensor_tensor(diff[:], th[:], 3.0, diff[:], ALU.add, ALU.mult).then_inc(u_done, 1)
                    if u == 24 and pre:
                        dve.wait_ge(x1_copied, KT * p + KT)
                        if post:
                            dve.wait_ge(gate_mm, 2 * q)
                        vec.tensor_copy(x1_hi[:, nxt], x1_t[:, nxt]).then_inc(x1_hi_done, 1)
                        dve.wait_ge(x1_hi_done, p + 1)
                        vec.tensor_tensor(x1_lo[:, nxt], x1_t[:, nxt], x1_hi[:, nxt].bitcast(F32),
                                          ALU.subtract).then_inc(x1_lo_done, 1)
                    if u == 24 and attend:
                        recip(b, 0, par)
                    if u in (20, 22, 25, 30) and ahead:
                        t = (20, 22, 25, 30).index(u)
                        if t == 0:
                            wait(dve, stored, 16 * q)
                        node_terms(b + 2, par, t)
                    if 26 <= u < 30 and pre:
                        n = u - 26
                        dve.wait_ge(qk_hi, 4 * p + n + 1)
                        vec.tensor_tensor(stage[:, n, 1], misc[(2, 1, 0, 2)[n]][:], stage[:, n, 0].bitcast(F32),
                                          ALU.subtract).then_inc(qk_lo, 1)
                    if u == 28 and attend:
                        normalise(b, 0)
                    if u == 30 and post:
                        for t in range(NT):
                            dve.wait_ge(y_turned, 2 * q + t // 2 + 1)
                            vec.bn_stats(stats[:, 1, t], misc[t // 2][:, t % 2 * H:t % 2 * H + H]).then_inc(stats2, 1)
                        for t in range(NT):
                            dve.wait_ge(stats2, NT * q + t + 1)
                            hold(dve)
                            vec.bn_aggr(mean_var[:, 1, t], stats[:, 1, t]).then_inc(aggr2, 1)
                    if u == 31 and post:
                        wait(dve, stored, 16 * q)
                        if ahead:
                            dve.wait_ge(f_done, 2 * NT * (b + 3))
                        dve.wait_ge(rstd2, 2 * q + 2)
                        for t in range(NT):
                            vec.tensor_scalar(y_out[:, t], misc[t // 2][:, t % 2 * H:t % 2 * H + H],
                                              mean_var[:, 1, t, 0:1], rstd[:, 1, t:t + 1],
                                              ALU.subtract, ALU.mult).then_inc(applied, 1)

            run(dve, step)

        @block.scalar
        def _(act):
            fun = nc.scalar.activation

            def copy_turned(b, u):
                qq, j, r, h, qt = unit(u)
                act.wait_ge(p_turned, U * b + u + 1)
                wait(act, c_mm, 4 * b + qq - 1)
                nc.scalar.copy(probs_t[:, qq % 2, j, :, r * P:r * P + P],
                               ps_t[u % 2][:].rearrange("p (k q) -> p k q", k=NT)).then_inc(p_scalar, 1)

            def copy_recip(b, half, bank):
                act.wait_ge(rec_rows, 2 * b + half + 1)
                wait(act, c_done, 2 * b + half)
                nc.scalar.copy(recip_b[:], bank[:]).then_inc(rec_copied, 1)

            def step(b, attend, pre, post, ahead, parity=None):
                par = b % 2 if parity is None else parity
                nxt = 1 - par
                p, q = b + 1, b - 1
                for u in range(U):
                    if attend:
                        qq, j, r, h, qt = unit(u)
                        wait(act, p_turned, U * b + u - 1)
                        act.wait_ge(s_masked, U * b + u + 1)
                        fun(probs[:, u % 2], ps_s[u % 2][:], ACT.Exp, bias=s_min[:, u:u + 1], scale=-1.0,
                            accum_out=s_sum[:, h, qt:qt + 1]).then_inc(s_exp, 1)
                    if u >= 3 and not by_vector(u - 3) and attend:
                        copy_turned(b, u - 3)
                    if u < 3 and not by_vector(u - 3 + U) and post:
                        copy_turned(q, u - 3 + U)

                    if u == 5 and post:
                        copy_recip(q, 1, misc[1])
                    if 6 <= u < 10 and pre:
                        t = u - 6
                        if t == 0:
                            act.wait_ge(z_bias_done, p + 1)
                            wait(act, z_rec_done, p)
                        act.wait_ge(z_leaky, NT * p + t + 1)
                        fun(z[:, t], z[:, t], ACT.Exp, bias=z_bias[:, t:t + 1],
                            accum_out=z_sum[:, t:t + 1]).then_inc(z_exp, 1)
                    if 9 <= u < 13 and pre:
                        t = u - 9
                        if t == 0:
                            wait(act, agg_done, 2 * p)
                        act.wait_ge(z_turned, NT * p + t + 1)
                        nc.scalar.copy(z_t[:, :, t * P:t * P + P],
                                       misc[2 - t % 2][:].rearrange("p (m n) -> p m n", m=NT)).then_inc(z_copied, 1)
                    if u in (10, 12) and attend:
                        n = (u - 10) // 2
                        if n == 0:
                            wait(act, c_mm, 4 * b)
                        act.wait_ge(v_mm, 2 * b + n + 1)
                        nc.scalar.copy(v[:, 2 * n:2 * n + 2],
                                       misc[0][:].rearrange("p (t i) -> p t i", t=2)).then_inc(v_done, 1)
                    if u in (14, 16) and pre:
                        n = (u - 14) // 2
                        act.wait_ge(agg_done, 2 * p + n + 1)
                        act.wait_ge(z_rec_done, p + 1)
                        wait(act, x1_turned, KT * p)
                        for t in (2 * n, 2 * n + 1):
                            fun(hx[:, t], misc[2 - n][:, t % 2 * H:t % 2 * H + H], ACT.Identity,
                                scale=z_rec[:, t:t + 1]).then_inc(h_done, 1)
                        if n == 1:
                            act.wait_ge(h_done, NT * p + NT)
                            wait(act, x1_done, NT * p)
                            fun(ey[:], hx[:], ACT.Exp).then_inc(e_done, 1)
                    if u in (18, 20) and post:
                        oh = (u - 18) // 2
                        act.wait_ge(gate_mm, 2 * q + oh + 1)
                        wait(act, u_done, q)
                        fun(th[:, oh], misc[2 * oh][:], ACT.Tanh, bias=half_b[:, oh:oh + 1],
                            scale=0.5).then_inc(tanh_done, 1)
                    if u == 23 and pre:
                        for kt in range(KT):
                            act.wait_ge(x1_turned, KT * p + kt + 1)
                            if post:
                                act.wait_ge(ds_done, 2 * b)
                            nc.scalar.copy(x1_t[:, nxt, kt], misc[1 - kt][:]).then_inc(x1_copied, 1)
                    if 25 <= u < 29 and pre:
                        n = u - 25
                        act.wait_ge(qk_mm, 4 * p + n + 1)
                        wait(act, s_mm, U * b + (Q if n < 2 else 3 * Q))
                        nc.scalar.copy(stage[:, n, 0], misc[(2, 1, 0, 2)[n]][:]).then_inc(qk_hi, 1)
                    if u == 28 and attend:
                        copy_recip(b, 0, misc[1])

            act.wait_ge(half_done, 2)
            run(act, step)

        @block.gpsimd
        def _(pool):
            gp = nc.gpsimd

            def inverse_std(which, eps, done, base):
                gp.tensor_scalar(var_eps[:, which], mean_var[:, which, :, 1], eps, 1.0, ALU.add,
                                 ALU.mult).then_inc(done, 1)
                pool.wait_ge(done, base + 1)
                gp.tensor_tensor(rstd[:, which], var_eps[:, which], neg_half[:], ALU.pow).then_inc(done, 1)

            pool.wait_ge(half_done, 2)

            def step(b, attend, pre, post, ahead, parity=None):
                par = b % 2 if parity is None else parity
                nxt, prv = 1 - par, 1 - par
                p, q = b + 1, b - 1
                if pre:
                    for t in range(NT):
                        pool.wait_ge(z_masked, NT * p + t + 1)
                        hold(pool)
                        gp.tensor_scalar(z[:, t], z[:, t], f12[:, nxt, 0, t:t + 1], 1.0, ALU.add,
                                         ALU.mult).then_inc(z_added, 1)
                if post:
                    pool.wait_ge(c_done, 2 * b)
                    wait(pool, y2_done, q)
                    wait(pool, y_turned, 2 * q)
                    gp.tensor_tensor(diff[:], x1_t[:, prv], c_t[:], ALU.subtract).then_inc(ds_done, 1)
                    gp.tensor_scalar(summ[:], c_t[:], 4.0, 0.0, ALU.mult, ALU.add).then_inc(ds_done, 1)
                if pre:
                    pool.wait_ge(aggr1, NT * p + NT)
                    hold(pool)
                    gp.tensor_scalar(neg_mean[:], mean_var[:, 0, :, 0], -1.0, 0.0, ALU.mult, ALU.add).then_inc(rstd1, 1)
                    inverse_std(0, EPS, rstd1, 3 * p + 1)
                    pool.wait_ge(rstd1, 3 * p + 3)
                    hold(pool)
                    for t in range(NT):
                        gp.tensor_scalar(hx[:, t], ey[:, t], neg_mean[:, t:t + 1], rstd[:, 0, t:t + 1], ALU.add,
                                         ALU.mult).then_inc(x1_done, 1)
                if post:
                    pool.wait_ge(u_done, b)
                    gp.tensor_tensor(summ[:], summ[:], diff[:], ALU.add).then_inc(y2_done, 1)
                    pool.wait_ge(aggr2, NT * b)
                    hold(pool)
                    inverse_std(1, 4 * EPS, rstd2, 2 * q)

            run(pool, step)


def kernel(**inputs):
    import numpy as _np
    import concourse.bacc as _bacc
    from concourse.bass_utils import run_bass_kernel_spmd as _run

    given = {
        "x": inputs["x"],
        "adj": inputs["adj"],
        "w_fc": inputs["L0_gnn_W_fc"],
        "w_attn": _np.asarray(inputs["L0_gnn_W_attn"]).reshape(2, -1).T,
        "wq_t": _np.asarray(inputs["L1_gnn_Wq"]).T,
        "wk_t": _np.asarray(inputs["L1_gnn_Wk"]).T,
        "wv_t": _np.asarray(inputs["L1_gnn_Wv"]).T,
        "wg_t": _np.asarray(inputs["L1_gnn_Wg"]).T,
        "bg": _np.asarray(inputs["L1_gnn_bg"]).reshape(-1, P).T,
        "eye": _np.eye(P, dtype=_np.float32),
    }
    nc = _bacc.Bacc("TRN2", target_bir_lowering=False, num_devices=1)
    arrays, args = {}, []
    for name, a in given.items():
        a = _np.ascontiguousarray(a)
        arrays[name] = a
        args.append(nc.dram_tensor(name, a.shape, mybir.dt.from_np(a.dtype), kind="ExternalInput").ap())
    shape = given["x"].shape
    args.append(nc.dram_tensor("out", shape, F32, kind="ExternalOutput").ap())
    two_layer_gat(nc, *args)
    r = _run(nc, [arrays], core_ids=[0])
    return r.results[0]["out"]
```

```python
from contextlib import ExitStack

import concourse.bass as bass
from concourse import mybir

ALU = mybir.AluOpType
ACT = mybir.ActivationFunctionType
F32 = mybir.dt.float32
F32R = mybir.dt.float32r
BF16 = mybir.dt.bfloat16
I32 = mybir.dt.int32

P = 128
NH = 8
MASKED = -1e30
EPS = 1e-5
SLOPE = 0.2
BIG = 3e38


def two_layer_gat(nc, x, adj, w_fc, w_attn, wq_t, wk_t, wv_t, wg_t, bg, eye, out):
    B, N, H = x.shape
    NT = N // P
    KT = H // P
    DK = H // NH
    HPH = P // DK
    OF = w_fc.shape[0]
    SCALE = float(DK) ** -0.5
    U = NH * NT
    Q = U // 4
    PARTS = P // DK
    PACK = 16 * PARTS
    assert (N, H, NT, KT, DK, HPH, U, B % 2) == (512, 256, 4, 2, 32, 4, 32, 0)

    def unit(u):
        qq, j, r = u // Q, u % Q // 2, u % 2
        return qq, j, r, qq // 2 * HPH + j, qq % 2 * 2 + r

    def by_vector(u):
        return u % 4 == 3

    def vector_copies(u):
        return (u + 1) // 4

    def scalar_copies(u):
        return u + 1 - vector_copies(u)

    def wait(eng, sem, value):
        if not (isinstance(value, int) and value <= 0):
            eng.wait_ge(sem, value)

    def hold(eng):
        eng.nop(nofuse=True)

    with ExitStack() as ctx:
        def sb(name, shape, dt=F32):
            return ctx.enter_context(nc.sbuf_tensor(name, shape, dt))

        def sem(name):
            return ctx.enter_context(nc.semaphore(name))

        x_in = sb("x_in", [P, 2, NT, H])
        adj_in = sb("adj_in", [P, NT, N], I32)
        mask_add = sb("mask_add", [P, 2, NT, N], BF16)
        z = sb("z", [P, NT, N])
        z_t = sb("z_t", [P, NT, N])
        hx = sb("hx", [P, NT, H])
        ey = sb("ey", [P, NT, H])
        x1_t = sb("x1_t", [P, 2, KT, N])
        x1_hi = sb("x1_hi", [P, 2, KT, N], F32R)
        x1_lo = sb("x1_lo", [P, 2, KT, N], F32R)
        stage = sb("stage", [P, 8, N], F32R)
        qk_pack = sb("qk_pack", [P, NH, 2, N], F32R)
        v = sb("v", [P, NT, H])
        probs = sb("probs", [P, 2, N])
        probs_t = sb("probs_t", [P, 2, HPH, NT, 2 * P])
        recip_b = sb("recip_b", [P, N])
        c_t = sb("c_t", [P, 2, N])
        th = sb("th", [P, KT, N])
        diff = sb("diff", [P, KT, N])
        summ = sb("summ", [P, KT, N])
        y_out = sb("y_out", [P, NT, H])
        w_hi = sb("w_hi", [P, 4, KT, H], F32R)
        w_lo = sb("w_lo", [P, 4, KT, H], F32R)
        w_gc = sb("w_gc", [P, KT, H])
        wf = sb("wf", [P, 2, H])
        ident = sb("ident", [P, P])
        fc_in = y_out[0:OF, 0]
        attn_in = sb("attn_in", [OF, 2])
        gate_b = sb("gate_b", [P, KT])
        half_b = sb("half_b", [P, KT])
        f12 = sb("f12", [P, 2, 2, NT])
        z_max = sb("z_max", [P, NT])
        z_nmf = sb("z_nmf", [P, NT])
        z_bias = sb("z_bias", [P, NT])
        z_sum = sb("z_sum", [P, NT])
        z_rec = sb("z_rec", [P, NT])
        valid = sb("valid", [P, 2, NT])
        s_min = sb("s_min", [P, U])
        s_sum = sb("s_sum", [P, NH, NT])
        s_val = sb("s_val", [P, NH, NT])
        s_rec = sb("s_rec", [P, NH, NT])
        s_wide = sb("s_wide", [P, NT, HPH, DK])
        stats = sb("stats", [P, 2, NT, 6])
        mean_var = sb("mean_var", [P, 2, NT, 2])
        var_eps = sb("var_eps", [P, 2, NT])
        rstd = sb("rstd", [P, 2, NT])
        neg_mean = sb("neg_mean", [P, NT])
        mean_rstd = sb("mean_rstd", [P, NT])
        neg_half = sb("neg_half", [P, NT])

        ps_s = [ctx.enter_context(nc.psum_tensor(f"ps_s{k}", [P, N], F32)) for k in range(2)]
        ps_t = [ctx.enter_context(nc.psum_tensor(f"ps_t{k}", [P, N], F32)) for k in range(2)]
        ps_c = ctx.enter_context(nc.psum_tensor("ps_c", [P, N], F32))
        misc = [ctx.enter_context(nc.psum_tensor(f"misc{k}", [P, N], F32)) for k in range(3)]

        weights_in = sem("weights_in")
        consts_in = sem("consts_in")
        w_hi_done = sem("w_hi_done")
        w_lo_done = sem("w_lo_done")
        wf_mm = sem("wf_mm")
        wf_done = sem("wf_done")
        half_done = sem("half_done")
        x_loaded = sem("x_loaded")
        adj_loaded = sem("adj_loaded")
        packed = [sem(f"packed{h}") for h in range(NH)]
        stored = sem("stored")
        f_done = sem("f_done")
        mask_done = sem("mask_done")
        f2_rows = sem("f2_rows")
        z_masked = sem("z_masked")
        z_added = sem("z_added")
        z_leaky = sem("z_leaky")
        z_nmf_done = sem("z_nmf_done")
        z_bias_done = sem("z_bias_done")
        z_exp = sem("z_exp")
        z_turned = sem("z_turned")
        z_copied = sem("z_copied")
        z_rec_done = sem("z_rec_done")
        agg_done = sem("agg_done")
        h_done = sem("h_done")
        e_done = sem("e_done")
        res_done = sem("res_done")
        y1_done = sem("y1_done")
        stats1 = sem("stats1")
        aggr1 = sem("aggr1")
        rstd1 = sem("rstd1")
        x1_done = sem("x1_done")
        x1_turned = sem("x1_turned")
        x1_copied = sem("x1_copied")
        x1_hi_done = sem("x1_hi_done")
        x1_lo_done = sem("x1_lo_done")
        qk_mm = sem("qk_mm")
        qk_hi = sem("qk_hi")
        qk_lo = sem("qk_lo")
        v_mm = sem("v_mm")
        v_done = sem("v_done")
        s_mm = sem("s_mm")
        s_masked = sem("s_masked")
        s_exp = sem("s_exp")
        p_turned = sem("p_turned")
        p_scalar = sem("p_scalar")
        p_vector = sem("p_vector")
        c_mm = sem("c_mm")
        sum_valid = sem("sum_valid")
        rec_done = sem("rec_done")
        rec_wide = sem("rec_wide")
        rec_rows = sem("rec_rows")
        rec_copied = sem("rec_copied")
        c_done = sem("c_done")
        gate_mm = sem("gate_mm")
        tanh_done = sem("tanh_done")
        ds_done = sem("ds_done")
        u_done = sem("u_done")
        y2_done = sem("y2_done")
        y_turned = sem("y_turned")
        stats2 = sem("stats2")
        aggr2 = sem("aggr2")
        rstd2 = sem("rstd2")
        applied = sem("applied")

        block = ctx.enter_context(nc.Block())

        def run(eng, step):
            def apart(b):
                step(b, attend=0 <= b < B, pre=b < B - 1, post=1 <= b <= B, late=b >= 2, ahead=b < B - 2)

            for b in range(-1, 3):
                apart(b)
            with eng.Fori(0, (B - 6) // 2) as i:
                for k in range(2):
                    step(2 * i + 3 + k, attend=True, pre=True, post=True, late=True, ahead=True, parity=(3 + k) % 2)
            for b in range(B - 3, B + 2):
                apart(b)

        @block.sync
        def _(sp):
            sp.dma_start(ident[:], eye).then_inc(consts_in, 16)
            sp.dma_start(fc_in, w_fc).then_inc(consts_in, 16)
            sp.dma_start(attn_in[:], w_attn).then_inc(consts_in, 16)
            sp.dma_start(gate_b[:], bg).then_inc(consts_in, 16)

            def load_x(g, par):
                src = x[bass.ds(g, 1)].rearrange("g (t p) i -> p (g t) i", p=P)
                sp.dma_start(x_in[:, par], src).then_inc(x_loaded, 16)

            def load_adj(g):
                src = adj[bass.ds(g, 1)].rearrange("g (t p) m -> p (g t) m", p=P)
                sp.dma_start(adj_in[:], src).then_inc(adj_loaded, 16)

            load_x(0, 0)
            load_adj(0)
            raw = probs_t[:].rearrange("p a h k q -> p (a h k) q")
            for n, w in enumerate((wq_t, wk_t, wv_t)):
                sp.dma_start(raw[:, KT * n:KT * n + KT], w.rearrange("(t p) o -> p t o", p=P)).then_inc(weights_in, 16)
            sp.dma_start(raw[:, 3 * KT:4 * KT], wg_t[H:2 * H].rearrange("(t p) o -> p t o", p=P)).then_inc(weights_in, 16)
            sp.dma_start(w_gc[:], wg_t[0:H].rearrange("(t p) o -> p t o", p=P)).then_inc(weights_in, 16)

            def pack_head(half, j):
                h = half * HPH + j
                rows = slice(j * DK, j * DK + DK)
                for part in range(PARTS):
                    q_lo, k_lo = part // 2, part % 2
                    first, second = 4 * half + q_lo, 4 * half + 2 + k_lo
                    sp.dma_start(qk_pack[part * DK:part * DK + DK, h].bitcast(F32),
                                 stage[rows, first:second + 1:second - first].bitcast(F32)).then_inc(packed[h], 16)

            def step(b, attend, pre, post, late, ahead, parity=None):
                par = b % 2 if parity is None else parity
                if ahead:
                    wait(sp, res_done, 2 * b + 2)
                    hold(sp)
                    load_x(b + 2, par)
                if ahead:
                    wait(sp, mask_done, 2 * b + 4)
                    hold(sp)
                    load_adj(b + 2)
                if late:
                    sp.wait_ge(applied, NT * (b - 1))
                    hold(sp)
                    dst = out[bass.ds(b - 2, 1)].rearrange("g (t p) i -> p (g t) i", p=P)
                    sp.dma_start(dst, y_out[:]).then_inc(stored, 16)
                if attend:
                    for j in range(HPH):
                        if j == 0:
                            sp.wait_ge(qk_lo, 4 * b + 4)
                            hold(sp)
                        wait(sp, s_mm, U * (b - 1) + 3 * Q + 2 * j + 2)
                        pack_head(1, j)
                if pre:
                    for j in range(HPH):
                        if j == 0:
                            sp.wait_ge(qk_lo, 4 * (b + 1) + 2)
                            hold(sp)
                        wait(sp, s_mm, U * b + Q + 2 * j + 2)
                        pack_head(0, j)

            run(sp, step)
            sp.wait_ge(stored, 16 * B)

        @block.tensor
        def _(pe):
            mm = nc.tensor.matmul

            pe.wait_ge(consts_in, 64)
            for a in range(2):
                last = mm(misc[0][:, a * H:a * H + H], attn_in[:, a:a + 1].to_broadcast([OF, P]), fc_in,
                          start=True, stop=True)
            last.then_inc(wf_mm, 1)

            def scores(b, u):
                qq, j, r, h, qt = unit(u)
                if qq % 2 == 0 and r == 0:
                    pe.wait_ge(packed[h], PACK * (b + 1))
                wait(pe, s_exp, U * b + u - 1)
                mm(ps_s[u % 2][:], qk_pack[:, h, 0, qt * P:qt * P + P], qk_pack[:, h, 1],
                   start=True, stop=True).then_inc(s_mm, 1)

            def turn(b, u):
                if u >= 2:
                    if by_vector(u - 2):
                        wait(pe, p_vector, U // 4 * b + vector_copies(u - 2))
                    else:
                        wait(pe, p_scalar, 3 * U // 4 * b + scalar_copies(u - 2))
                else:
                    if by_vector(u - 2 + U):
                        wait(pe, p_vector, U // 4 * (b - 1) + vector_copies(u - 2 + U))
                    else:
                        wait(pe, p_scalar, 3 * U // 4 * (b - 1) + scalar_copies(u - 2 + U))
                pe.wait_ge(s_exp, U * b + u + 1)
                for kt in range(NT):
                    last = nc.tensor.transpose(ps_t[u % 2][:, kt * P:kt * P + P],
                                               probs[:, u % 2, kt * P:kt * P + P], ident[:])
                last.then_inc(p_turned, 1)

            def attend_v(b, qq, kt):
                half, qh = qq // 2, qq % 2
                if kt == 0:
                    u = qq * Q + Q - 1
                    pe.wait_ge(p_vector, U // 4 * b + vector_copies(u))
                    pe.wait_ge(p_scalar, 3 * U // 4 * b + scalar_copies(u))
                    if qq == 0:
                        pe.wait_ge(v_done, 2 * b + 2)
                    if qh == 0:
                        wait(pe, c_done, 2 * b + half)
                for j in range(HPH):
                    h = half * HPH + j
                    last = mm(ps_c[j * DK:j * DK + DK, qh * 2 * P:qh * 2 * P + 2 * P], v[:, kt, h * DK:h * DK + DK],
                              probs_t[:, qq % 2, j, kt], start=(kt == 0), stop=(kt == NT - 1))
                if kt == NT - 1:
                    last.then_inc(c_mm, 1)

            def recip_rows(b, half, bank):
                pe.wait_ge(rec_wide, 2 * b + half + 1)
                for qt in range(NT):
                    last = nc.tensor.transpose(bank[:, qt * P:qt * P + P], s_wide[:, qt].rearrange("p j d -> p (j d)"),
                                               ident[:])
                last.then_inc(rec_rows, 1)

            def split_mm(dst, pairs, start=True, stop=True):
                for n, (a, c) in enumerate(pairs):
                    last = mm(dst, a, c, start=start and n == 0, stop=stop and n == len(pairs) - 1)
                return last

            def step(b, attend, pre, post, late, ahead, parity=None):
                par = b % 2 if parity is None else parity
                nxt, prv = 1 - par, 1 - par
                p, q = b + 1, b - 1
                for u in range(U):
                    if attend:
                        scores(b, u)
                    if u >= 2 and attend:
                        turn(b, u - 2)
                    if u < 2 and post:
                        turn(q, u - 2 + U)
                    if u >= 11 and (u - 11) % 8 < 4 and attend:
                        attend_v(b, (u - 11) // 8, (u - 11) % 8)
                    if 3 <= u < 7 and post:
                        attend_v(q, 3, u - 3)

                    if u == 0 and attend:
                        pe.wait_ge(qk_lo, 4 * b + 4)
                    if u == 0 and pre:
                        if isinstance(p, int) and p == 0:
                            pe.wait_ge(wf_done, 1)
                        pe.wait_ge(f_done, 2 * NT * p + 2 * NT)
                        for t in range(NT):
                            last = nc.tensor.transpose(misc[0][:, t * P:t * P + P],
                                                       f12[:, nxt, 1, t:t + 1].to_broadcast([P, P]), ident[:])
                        last.then_inc(f2_rows, 1)
                    if u == 4 and post:
                        wait(pe, applied, NT * q)
                        recip_rows(q, 1, misc[2])
                    if 3 <= u < 7 and attend:
                        t = u - 3
                        if t == 0:
                            wait(pe, applied, NT * q)
                            pe.wait_ge(x1_lo_done, KT * b + KT)
                        if t == 2 and pre:
                            pe.wait_ge(z_masked, NT * p + NT)
                        rows = slice(t * P, t * P + P)
                        pairs = [(a[:, par, kt, rows], w[:, 2, kt]) for kt in range(KT)
                                 for a, w in ((x1_hi, w_hi), (x1_hi, w_lo), (x1_lo, w_hi))]
                        last = split_mm(misc[1 - t // 2][:, t % 2 * H:t % 2 * H + H], pairs)
                        if t % 2 == 1:
                            last.then_inc(v_mm, 1)
                    if 7 <= u < 11 and pre:
                        t = u - 7
                        if t == 0 and post:
                            pe.wait_ge(rec_copied, 2 * b)
                        if t == 1 and attend:
                            pe.wait_ge(v_done, 2 * b + 1)
                        if t >= 2:
                            pe.wait_ge(z_copied, NT * p + t - 1)
                        pe.wait_ge(z_exp, NT * p + t + 1)
                        bank = misc[2 - t % 2]
                        for mt in range(NT):
                            last = nc.tensor.transpose(bank[:, mt * P:mt * P + P], z[:, t, mt * P:mt * P + P], ident[:])
                        last.then_inc(z_turned, 1)
                    if 10 <= u < 18 and pre:
                        t = (u - 10) // 2
                        mts = range(NT)[(u - 10) % 2 * 2:][:2]
                        if u == 10 and attend:
                            pe.wait_ge(v_done, 2 * b + 2)
                        if u == 10 and not attend:
                            pe.wait_ge(z_masked, NT * p + NT)
                        if u == 14:
                            pe.wait_ge(z_copied, NT * p + 4)
                        if mts[0] == 0 and t != 2:
                            pe.wait_ge(z_copied, NT * p + t + 1)
                        bank = misc[t // 2]
                        for mt in mts:
                            last = mm(bank[:, t % 2 * H:t % 2 * H + H], z_t[:, mt, t * P:t * P + P], x_in[:, nxt, mt],
                                      start=(mt == 0), stop=(mt == NT - 1))
                        if u in (13, 17):
                            last.then_inc(agg_done, 1)
                    if u in (15, 18) and post:
                        oh = (u - 15) // 3
                        if oh == 0 and not pre:
                            pe.wait_ge(rec_copied, 2 * b)
                        if oh == 1:
                            if pre:
                                pe.wait_ge(h_done, NT * p + 2)
                            elif attend:
                                pe.wait_ge(v_done, 2 * b + 2)
                        cols = slice(oh * P, oh * P + P)
                        pairs = [(w[:, 3, kt, cols], a[:, prv, kt]) for kt in range(KT)
                                 for w, a in ((w_hi, x1_hi), (w_lo, x1_hi), (w_hi, x1_lo))]
                        split_mm(misc[2 - 2 * oh][:], pairs, stop=False)
                    if u in (16, 19) and post:
                        oh = (u - 16) // 3
                        if oh == 0:
                            pe.wait_ge(c_done, 2 * b)
                        cols = slice(oh * P, oh * P + P)
                        pairs = [(w_gc[:, kt, cols], c_t[:, kt]) for kt in range(KT)]
                        split_mm(misc[2 - 2 * oh][:], pairs, start=False).then_inc(gate_mm, 1)
                    if u == 21 and attend:
                        if post:
                            pe.wait_ge(tanh_done, 2 * q + 1)
                        recip_rows(b, 0, misc[2])
                    if u == 23 and pre:
                        for kt in range(KT):
                            if kt == 0:
                                pe.wait_ge(h_done, NT * p + NT)
                                pe.wait_ge(x1_done, NT * p + NT)
                            elif attend:
                                pe.wait_ge(rec_copied, 2 * b + 1)
                            for t in range(NT):
                                last = nc.tensor.transpose(misc[1 + kt][:, t * P:t * P + P],
                                                           hx[:, t, kt * P:kt * P + P], ident[:])
                            last.then_inc(x1_turned, 1)
                    if 25 <= u < 29 and pre:
                        n = u - 25
                        if n == 0:
                            pe.wait_ge(x1_lo_done, KT * p + KT)
                            if post:
                                pe.wait_ge(tanh_done, 2 * q + 2)
                        if n == 3:
                            pe.wait_ge(qk_lo, 4 * p + 1)
                        cols = slice(n // 2 * P, n // 2 * P + P)
                        w0 = n % 2
                        pairs = [(w[:, w0, kt, cols], a[:, nxt, kt]) for kt in range(KT)
                                 for w, a in ((w_hi, x1_hi), (w_lo, x1_hi), (w_hi, x1_lo))]
                        split_mm(misc[n % 3][:], pairs).then_inc(qk_mm, 1)
                    if u in (29, 30) and post:
                        n = u - 29
                        if n == 0:
                            pe.wait_ge(y2_done, b)
                        if pre:
                            pe.wait_ge(qk_lo, 4 * p + 2 + n)
                        elif n == 0 and attend:
                            pe.wait_ge(v_done, 2 * b + 1)
                        elif n == 1 and attend:
                            pe.wait_ge(rec_copied, 2 * b + 1)
                        elif n == 1:
                            pe.wait_ge(tanh_done, 2 * q + 1)
                        for t in (2 * n, 2 * n + 1):
                            for kt in range(KT):
                                last = nc.tensor.transpose(
                                    misc[1 + n][:, t % 2 * H + kt * P:t % 2 * H + kt * P + P],
                                    summ[:, kt, t * P:t * P + P], ident[:])
                        last.then_inc(y_turned, 1)

            pe.wait_ge(w_lo_done, 4)
            run(pe, step)

        @block.vector
        def _(dve):
            vec = nc.vector
            raw = probs_t[:].rearrange("p a h k q -> p (a h k) q")
            vec.memset(neg_half[:], -0.5).then_inc(half_done, 1)
            dve.wait_ge(consts_in, 64)
            vec.tensor_scalar(half_b[:], gate_b[:], 0.5, None, ALU.mult).then_inc(half_done, 1)
            dve.wait_ge(wf_mm, 1)
            vec.tensor_copy(wf[:], misc[0][:].rearrange("p (a i) -> p a i", a=2)).then_inc(wf_done, 1)
            dve.wait_ge(wf_done, 1)
            dve.wait_ge(weights_in, 80)
            for n in range(4):
                vec.tensor_copy(w_hi[:, n], raw[:, KT * n:KT * n + KT]).then_inc(w_hi_done, 1)
                dve.wait_ge(w_hi_done, n + 1)
                vec.tensor_tensor(w_lo[:, n], raw[:, KT * n:KT * n + KT], w_hi[:, n].bitcast(F32),
                                  ALU.subtract).then_inc(w_lo_done, 1)
            dve.wait_ge(w_lo_done, 4)

            def node_terms(g, par, t):
                if t == 0:
                    dve.wait_ge(x_loaded, 16 * g + 16)
                for a in range(2):
                    wait(dve, f_done, 2 * NT * g + 2 * t + a - 1)
                    vec.tensor_tensor_reduce(y_out[:, (2 * t + a) % 2], x_in[:, par, t], wf[:, a], 1.0, 0.0,
                                             ALU.mult, ALU.add, f12[:, par, a, t:t + 1]).then_inc(f_done, 1)

            def copy_turned(b, u):
                qq, j, r, h, qt = unit(u)
                dve.wait_ge(p_turned, U * b + u + 1)
                wait(dve, c_mm, 4 * b + qq - 1)
                vec.tensor_copy(probs_t[:, qq % 2, j, :, r * P:r * P + P],
                                ps_t[u % 2][:].rearrange("p (k q) -> p k q", k=NT)).then_inc(p_vector, 1)

            def recip(b, half, par):
                hs = slice(half * HPH, half * HPH + HPH)
                dve.wait_ge(s_exp, U * b + U // 2 * (half + 1))
                vec.tensor_tensor(s_val[:, hs], s_sum[:, hs],
                                  valid[:, par].unsqueeze(1).to_broadcast([P, HPH, NT]), ALU.mult).then_inc(sum_valid, 1)
                dve.wait_ge(sum_valid, 2 * b + half + 1)
                vec.reciprocal(s_rec[:, hs], s_val[:, hs]).then_inc(rec_done, 1)
                dve.wait_ge(rec_done, 2 * b + half + 1)
                wait(dve, rec_rows, 2 * b + half)
                vec.tensor_copy(s_wide[:], s_rec[:, hs].rearrange("p j t -> p t j").unsqueeze(3)
                                .to_broadcast([P, NT, HPH, DK])).then_inc(rec_wide, 1)

            def normalise(b, half):
                dve.wait_ge(c_mm, 4 * b + 2 * half + 2)
                dve.wait_ge(rec_copied, 2 * b + half + 1)
                wait(dve, gate_mm, 2 * b)
                wait(dve, ds_done, 2 * b)
                vec.tensor_tensor(c_t[:, half], ps_c[:], recip_b[:], ALU.mult).then_inc(c_done, 1)

            def step(b, attend, pre, post, late, ahead, parity=None):
                par = b % 2 if parity is None else parity
                nxt, prv = 1 - par, 1 - par
                p, q = b + 1, b - 1
                if isinstance(b, int) and b == -1:
                    for t in range(NT):
                        node_terms(0, 0, t)
                for u in range(U):
                    if u >= 3 and by_vector(u - 3) and attend:
                        copy_turned(b, u - 3)
                    if u < 3 and by_vector(u - 3 + U) and post:
                        copy_turned(q, u - 3 + U)
                    if attend:
                        qt = unit(u)[4]
                        dve.wait_ge(s_mm, U * b + u + 1)
                        hold(dve)
                        vec.tensor_tensor_reduce(ps_s[u % 2][:], ps_s[u % 2][:], mask_add[:, par, qt], -SCALE, BIG,
                                                 ALU.add, ALU.min, s_min[:, u:u + 1]).then_inc(s_masked, 1)
                    if 1 <= u < 5 and pre:
                        t = u - 1
                        if t == 0:
                            wait(dve, z_turned, NT * p)
                            dve.wait_ge(f2_rows, p + 1)
                        dve.wait_ge(mask_done, 2 * p + t // 2 + 1)
                        hold(dve)
                        vec.tensor_tensor_reduce(z[:, t], misc[0][:], mask_add[:, nxt, t], 1.0, -BIG,
                                                 ALU.add, ALU.max, z_max[:, t:t + 1]).then_inc(z_masked, 1)
                    if u == 2 and post:
                        recip(q, 1, prv)
                    if u == 4 and pre:
                        dve.wait_ge(z_masked, NT * p + NT)
                        vec.scalar_tensor_tensor(z_nmf[:], z_max[:], -1.0, f12[:, nxt, 0], ALU.mult,
                                                 ALU.subtract).then_inc(z_nmf_done, 1)
                        vec.tensor_scalar(valid[:, nxt], z_max[:], MASKED / 10, None, ALU.is_gt).then_inc(z_nmf_done, 1)
                        dve.wait_ge(z_nmf_done, 2 * p + 2)
                        vec.scalar_tensor_tensor(z_bias[:], z_nmf[:], SLOPE, z_nmf[:], ALU.mult,
                                                 ALU.min).then_inc(z_bias_done, 1)
                    if 3 <= u < 7 and pre:
                        t = u - 3
                        dve.wait_ge(z_added, NT * p + t + 1)
                        vec.scalar_tensor_tensor(z[:, t], z[:, t], SLOPE, z[:, t], ALU.mult,
                                                 ALU.max).then_inc(z_leaky, 1)
                    if u == 7 and post:
                        normalise(q, 1)
                    if u == 9 and pre:
                        dve.wait_ge(z_exp, NT * p + NT)
                        vec.reciprocal(z_rec[:], z_sum[:]).then_inc(z_rec_done, 1)
                    if 9 <= u < 13 and ahead:
                        if u == 9:
                            wait(dve, stored, 16 * (b - 1))
                        node_terms(b + 2, par, u - 9)
                    if u in (15, 19) and pre:
                        n = (u - 15) // 4
                        pair = slice(2 * n, 2 * n + 2)
                        dve.wait_ge(e_done, 2 * p + n + 1)
                        dve.wait_ge(h_done, NT * p + 2 * n + 2)
                        vec.scalar_tensor_tensor(hx[:, pair], hx[:, pair], 0.0, x_in[:, nxt, pair],
                                                 ALU.max, ALU.add).then_inc(res_done, 1)
                        dve.wait_ge(res_done, 2 * p + n + 1)
                        vec.scalar_tensor_tensor(ey[:, pair], ey[:, pair], 1.0, hx[:, pair],
                                                 ALU.min, ALU.add).then_inc(y1_done, 1)
                    if u in (16, 20) and pre:
                        n = (u - 16) // 4
                        dve.wait_ge(y1_done, 2 * p + n + 1)
                        for t in (2 * n, 2 * n + 1):
                            vec.bn_stats(stats[:, 0, t], ey[:, t]).then_inc(stats1, 1)
                        wait(dve, x1_done, NT * p)
                        for t in (2 * n, 2 * n + 1):
                            dve.wait_ge(stats1, NT * p + t + 1)
                            hold(dve)
                            vec.bn_aggr(mean_var[:, 0, t], stats[:, 0, t]).then_inc(aggr1, 1)
                    if u == 17 and attend:
                        recip(b, 0, par)
                    if u == 21 and post:
                        dve.wait_ge(tanh_done, 2 * q + 2)
                        dve.wait_ge(ds_done, 2 * q + 2)
                        vec.scalar_tensor_tensor(diff[:], th[:], 3.0, diff[:], ALU.add, ALU.mult).then_inc(u_done, 1)
                    if u == 23 and pre:
                        if post:
                            dve.wait_ge(gate_mm, 2 * b)
                        for kt in range(KT):
                            dve.wait_ge(x1_copied, KT * p + kt + 1)
                            vec.tensor_copy(x1_hi[:, nxt, kt], x1_t[:, nxt, kt]).then_inc(x1_hi_done, 1)
                            dve.wait_ge(x1_hi_done, KT * p + kt + 1)
                            vec.tensor_tensor(x1_lo[:, nxt, kt], x1_t[:, nxt, kt], x1_hi[:, nxt, kt].bitcast(F32),
                                              ALU.subtract).then_inc(x1_lo_done, 1)
                    if u == 23 and attend:
                        normalise(b, 0)
                    if 27 <= u < 31 and pre:
                        n = u - 27
                        dve.wait_ge(qk_hi, 4 * p + n + 1)
                        vec.tensor_tensor(stage[:, 2 * n + 1], misc[n % 3][:], stage[:, 2 * n].bitcast(F32),
                                          ALU.subtract).then_inc(qk_lo, 1)
                    if u in (30, 31) and post:
                        n = u - 30
                        dve.wait_ge(y_turned, 2 * q + n + 1)
                        for t in (2 * n, 2 * n + 1):
                            vec.bn_stats(stats[:, 1, t], misc[1 + n][:, t % 2 * H:t % 2 * H + H]).then_inc(stats2, 1)
                        for t in (2 * n, 2 * n + 1):
                            dve.wait_ge(stats2, NT * q + t + 1)
                            hold(dve)
                            vec.bn_aggr(mean_var[:, 1, t], stats[:, 1, t]).then_inc(aggr2, 1)

            run(dve, step)

        @block.scalar
        def _(act):
            fun = nc.scalar.activation

            def copy_turned(b, u):
                qq, j, r, h, qt = unit(u)
                act.wait_ge(p_turned, U * b + u + 1)
                wait(act, c_mm, 4 * b + qq - 1)
                nc.scalar.copy(probs_t[:, qq % 2, j, :, r * P:r * P + P],
                               ps_t[u % 2][:].rearrange("p (k q) -> p k q", k=NT)).then_inc(p_scalar, 1)

            def copy_recip(b, half, bank):
                act.wait_ge(rec_rows, 2 * b + half + 1)
                wait(act, c_done, 2 * b + half)
                nc.scalar.copy(recip_b[:], bank[:]).then_inc(rec_copied, 1)

            def step(b, attend, pre, post, late, ahead, parity=None):
                par = b % 2 if parity is None else parity
                nxt = 1 - par
                p, q = b + 1, b - 1
                for u in range(U):
                    if u >= 3 and not by_vector(u - 3) and attend:
                        copy_turned(b, u - 3)
                    if u < 3 and not by_vector(u - 3 + U) and post:
                        copy_turned(q, u - 3 + U)
                    if attend:
                        qq, j, r, h, qt = unit(u)
                        wait(act, p_turned, U * b + u - 1)
                        act.wait_ge(s_masked, U * b + u + 1)
                        fun(probs[:, u % 2], ps_s[u % 2][:], ACT.Exp, bias=s_min[:, u:u + 1], scale=-1.0,
                            accum_out=s_sum[:, h, qt:qt + 1]).then_inc(s_exp, 1)
                    if u == 2 and late:
                        wait(act, stored, 16 * (b - 2))
                        act.wait_ge(f_done, 2 * NT * (min(b + 1, B) if isinstance(b, int) else b + 1))
                        act.wait_ge(rstd2, 4 * q)
                        for t in range(NT):
                            fun(y_out[:, t], misc[1 + t // 2][:, t % 2 * H:t % 2 * H + H], ACT.Identity,
                                bias=mean_rstd[:, t:t + 1], scale=rstd[:, 1, t:t + 1]).then_inc(applied, 1)
                    if u == 5 and post:
                        copy_recip(q, 1, misc[2])
                    if 5 <= u < 9 and pre:
                        t = u - 5
                        if t == 0:
                            act.wait_ge(z_bias_done, p + 1)
                            wait(act, z_rec_done, p)
                        act.wait_ge(z_leaky, NT * p + t + 1)
                        fun(z[:, t], z[:, t], ACT.Exp, bias=z_bias[:, t:t + 1],
                            accum_out=z_sum[:, t:t + 1]).then_inc(z_exp, 1)
                    if u in (7, 8) and attend:
                        n = u - 7
                        if n == 0:
                            wait(act, c_mm, 4 * b)
                        act.wait_ge(v_mm, 2 * b + n + 1)
                        nc.scalar.copy(v[:, 2 * n:2 * n + 2],
                                       misc[1 - n][:].rearrange("p (t i) -> p t i", t=2)).then_inc(v_done, 1)
                    if 8 <= u < 12 and pre:
                        t = u - 8
                        if t == 0:
                            wait(act, agg_done, 2 * p)
                        act.wait_ge(z_turned, NT * p + t + 1)
                        nc.scalar.copy(z_t[:, :, t * P:t * P + P],
                                       misc[2 - t % 2][:].rearrange("p (m n) -> p m n", m=NT)).then_inc(z_copied, 1)
                    if u in (14, 18) and pre:
                        n = (u - 14) // 4
                        pair = slice(2 * n, 2 * n + 2)
                        act.wait_ge(agg_done, 2 * p + n + 1)
                        act.wait_ge(z_rec_done, p + 1)
                        wait(act, x1_turned, KT * p)
                        for t in (2 * n, 2 * n + 1):
                            fun(hx[:, t], misc[n][:, t % 2 * H:t % 2 * H + H], ACT.Identity,
                                scale=z_rec[:, t:t + 1]).then_inc(h_done, 1)
                        act.wait_ge(h_done, NT * p + 2 * n + 2)
                        wait(act, x1_done, NT * p)
                        fun(ey[:, pair], hx[:, pair], ACT.Exp).then_inc(e_done, 1)
                    if u in (17, 20) and post:
                        oh = (u - 17) // 3
                        act.wait_ge(gate_mm, 2 * q + oh + 1)
                        wait(act, u_done, q)
                        fun(th[:, oh], misc[2 - 2 * oh][:], ACT.Tanh, bias=half_b[:, oh:oh + 1],
                            scale=0.5).then_inc(tanh_done, 1)
                    if u == 22 and attend:
                        copy_recip(b, 0, misc[2])
                    if u == 23 and pre:
                        for kt in range(KT):
                            act.wait_ge(x1_turned, KT * p + kt + 1)
                            if post:
                                act.wait_ge(ds_done, 2 * b)
                            nc.scalar.copy(x1_t[:, nxt, kt], misc[1 + kt][:]).then_inc(x1_copied, 1)
                    if 26 <= u < 30 and pre:
                        n = u - 26
                        act.wait_ge(qk_mm, 4 * p + n + 1)
                        wait(act, s_mm, U * b + (Q if n < 2 else 3 * Q))
                        nc.scalar.copy(stage[:, 2 * n], misc[n % 3][:]).then_inc(qk_hi, 1)

            act.wait_ge(half_done, 2)
            run(act, step)

        @block.gpsimd
        def _(pool):
            gp = nc.gpsimd

            def inverse_std(which, eps, done, base):
                gp.tensor_scalar(var_eps[:, which], mean_var[:, which, :, 1], eps, 1.0, ALU.add,
                                 ALU.mult).then_inc(done, 1)
                pool.wait_ge(done, base + 1)
                gp.tensor_tensor(rstd[:, which], var_eps[:, which], neg_half[:], ALU.pow).then_inc(done, 1)

            def mask(g, par, n):
                pool.wait_ge(adj_loaded, 16 * g + 16)
                wait(pool, s_masked, U * (g - 2) + (3 * Q if n == 0 else 4 * Q))
                wait(pool, z_masked, NT * (g - 2) + NT)
                hold(pool)
                pair = slice(2 * n, 2 * n + 2)
                gp.tensor_scalar(mask_add[:, par, pair], adj_in[:, pair], 0.0, MASKED,
                                 ALU.is_equal, ALU.mult).then_inc(mask_done, 1)

            pool.wait_ge(half_done, 2)

            def step(b, attend, pre, post, late, ahead, parity=None):
                par = b % 2 if parity is None else parity
                nxt, prv = 1 - par, 1 - par
                p, q = b + 1, b - 1
                if pre:
                    if isinstance(b, int) and b == -1:
                        mask(0, 0, 0)
                    mask(p, nxt, 1)
                    for t in range(NT):
                        pool.wait_ge(z_masked, NT * p + t + 1)
                        hold(pool)
                        gp.tensor_scalar(z[:, t], z[:, t], f12[:, nxt, 0, t:t + 1], 1.0, ALU.add,
                                         ALU.mult).then_inc(z_added, 1)
                if post:
                    pool.wait_ge(c_done, 2 * b)
                    wait(pool, y2_done, q)
                    wait(pool, y_turned, 2 * q)
                    gp.tensor_tensor(diff[:], x1_t[:, prv], c_t[:], ALU.subtract).then_inc(ds_done, 1)
                    gp.tensor_scalar(summ[:], c_t[:], 4.0, 0.0, ALU.mult, ALU.add).then_inc(ds_done, 1)
                if pre:
                    pool.wait_ge(aggr1, NT * p + NT)
                    hold(pool)
                    gp.tensor_scalar(neg_mean[:], mean_var[:, 0, :, 0], -1.0, 0.0, ALU.mult, ALU.add).then_inc(rstd1, 1)
                    inverse_std(0, EPS, rstd1, 3 * p + 1)
                    pool.wait_ge(rstd1, 3 * p + 3)
                    hold(pool)
                    for t in range(NT):
                        gp.tensor_scalar(hx[:, t], ey[:, t], neg_mean[:, t:t + 1], rstd[:, 0, t:t + 1], ALU.add,
                                         ALU.mult).then_inc(x1_done, 1)
                if post:
                    pool.wait_ge(u_done, b)
                    gp.tensor_tensor(summ[:], summ[:], diff[:], ALU.add).then_inc(y2_done, 1)
                if ahead:
                    mask(b + 2, par, 0)
                if post:
                    pool.wait_ge(aggr2, NT * b)
                    hold(pool)
                    inverse_std(1, 4 * EPS, rstd2, 4 * q)
                    wait(pool, applied, NT * q)
                    hold(pool)
                    gp.tensor_scalar(mean_rstd[:], mean_var[:, 1, :, 0], -1.0, 0.0, ALU.mult, ALU.add).then_inc(rstd2, 1)
                    pool.wait_ge(rstd2, 4 * q + 3)
                    gp.tensor_tensor(mean_rstd[:], mean_rstd[:], rstd[:, 1], ALU.mult).then_inc(rstd2, 1)

            run(pool, step)


def kernel(**inputs):
    import numpy as _np
    import concourse.bacc as _bacc
    from concourse.bass_utils import run_bass_kernel_spmd as _run

    given = {
        "x": inputs["x"],
        "adj": inputs["adj"],
        "w_fc": inputs["L0_gnn_W_fc"],
        "w_attn": _np.asarray(inputs["L0_gnn_W_attn"]).reshape(2, -1).T,
        "wq_t": _np.asarray(inputs["L1_gnn_Wq"]).T,
        "wk_t": _np.asarray(inputs["L1_gnn_Wk"]).T,
        "wv_t": _np.asarray(inputs["L1_gnn_Wv"]).T,
        "wg_t": _np.asarray(inputs["L1_gnn_Wg"]).T,
        "bg": _np.asarray(inputs["L1_gnn_bg"]).reshape(-1, P).T,
        "eye": _np.eye(P, dtype=_np.float32),
    }
    nc = _bacc.Bacc("TRN2", target_bir_lowering=False, num_devices=1)
    arrays, args = {}, []
    for name, a in given.items():
        a = _np.ascontiguousarray(a)
        arrays[name] = a
        args.append(nc.dram_tensor(name, a.shape, mybir.dt.from_np(a.dtype), kind="ExternalInput").ap())
    shape = given["x"].shape
    args.append(nc.dram_tensor("out", shape, F32, kind="ExternalOutput").ap())
    two_layer_gat(nc, *args)
    r = _run(nc, [arrays], core_ids=[0])
    return r.results[0]["out"]
```

```python
from contextlib import ExitStack

import concourse.bass as bass
from concourse import mybir

ALU = mybir.AluOpType
ACT = mybir.ActivationFunctionType
F32 = mybir.dt.float32
F32R = mybir.dt.float32r
BF16 = mybir.dt.bfloat16
I32 = mybir.dt.int32

P = 128
NH = 8
MASKED = -1e30
EPS = 1e-5
SLOPE = 0.2
BIG = 3e38


def two_layer_gat(nc, x, adj, w_fc, w_attn, wq_t, wk_t, wv_t, wg_t, bg, eye, out):
    B, N, H = x.shape
    NT = N // P
    KT = H // P
    DK = H // NH
    HPH = P // DK
    OF = w_fc.shape[0]
    SCALE = float(DK) ** -0.5
    U = NH * NT
    Q = U // 4
    PARTS = P // DK
    PACK = 16 * PARTS
    assert (N, H, NT, KT, DK, HPH, U, B % 2) == (512, 256, 4, 2, 32, 4, 32, 0)

    def unit(u):
        qq, j, r = u // Q, u % Q // 2, u % 2
        return qq, j, r, qq // 2 * HPH + j, qq % 2 * 2 + r

    PE_V = (11, 12, 13, 15, 20, 21, 21, 22, 27, 28, 30, 31, 36, 37, 37, 38)
    PE_ROWS1 = 5
    PE_PROJ_V = (4, 5, 6, 7)
    PE_TURN_Z = (8, 9, 10, 11)
    PE_AGG = (11, 12, 13, 14, 16, 17, 18, 19)
    PE_GATE_X = (16, 19)
    PE_GATE_C = (17, 21)
    PE_ROWS0 = 22
    PE_TURN_X = 23
    PE_PROJ_QK = (26, 27, 28, 29)
    PE_TURN_Y = (30, 31)
    DVE_MASK_Z = (1, 2, 3, 4)
    DVE_MASK_B = 1
    DVE_RECIP1 = 4
    DVE_BIAS = 4
    DVE_LEAKY = (4, 5, 6, 7)
    DVE_NORM1 = 7
    DVE_COPY_V = (9, 10)
    DVE_Z_REC = 10
    DVE_NODE = (12, 13, 14, 15)
    DVE_RES = (16, 20)
    DVE_STATS1 = (17, 21)
    DVE_RECIP0 = 19
    DVE_GATED = 26
    DVE_SPLIT_X = 24
    DVE_NORM0 = 23
    DVE_X1 = 22
    DVE_STAGE = (27, 28, 29, 30)
    DVE_STATS2 = (30, 31)
    ACT_APPLY = (2, 3)
    ACT_ROWS1 = 6
    ACT_EXP_Z = (5, 6, 8, 9)
    ACT_COPY_Z = (9, 10, 11, 12)
    ACT_AGG = (15, 19)
    ACT_TANH = (18, 21)
    ACT_ROWS0 = 22
    ACT_COPY_X = 23
    ACT_STAGE = (26, 27, 28, 29)
    BY_VECTOR = (0, 4, 6, 9, 13, 23)
    NV = len(BY_VECTOR)

    def by_vector(u):
        return u in BY_VECTOR

    def vector_copies(u):
        return sum(n <= u for n in BY_VECTOR)

    def scalar_copies(u):
        return u + 1 - vector_copies(u)

    def wait(eng, sem, value):
        if not (isinstance(value, int) and value <= 0):
            eng.wait_ge(sem, value)

    def hold(eng):
        eng.nop(nofuse=True)

    with ExitStack() as ctx:
        def sb(name, shape, dt=F32):
            return ctx.enter_context(nc.sbuf_tensor(name, shape, dt))

        def sem(name):
            return ctx.enter_context(nc.semaphore(name))

        x_in = sb("x_in", [P, 2, NT, H])
        adj_in = sb("adj_in", [P, NT, N], I32)
        mask_add = sb("mask_add", [P, 2, NT, N], BF16)
        z = sb("z", [P, NT, N])
        z_t = sb("z_t", [P, NT, N])
        hx = sb("hx", [P, NT, H])
        ey = sb("ey", [P, NT, H])
        x1_t = sb("x1_t", [P, 2, KT, N])
        x1_hi = sb("x1_hi", [P, 2, KT, N], F32R)
        x1_lo = sb("x1_lo", [P, 2, KT, N], F32R)
        stage = sb("stage", [P, 8, N], F32R)
        qk_pack = sb("qk_pack", [P, NH, 2, N], F32R)
        v = sb("v", [P, NT, H])
        probs = sb("probs", [P, 2, N])
        probs_t = sb("probs_t", [P, 2, HPH, NT, 2 * P])
        recip_b = sb("recip_b", [P, N])
        c_t = sb("c_t", [P, 2, N])
        th = sb("th", [P, KT, N])
        diff = sb("diff", [P, KT, N])
        summ = sb("summ", [P, KT, N])
        y_out = sb("y_out", [P, NT, H])
        w_hi = sb("w_hi", [P, 4, KT, H], F32R)
        w_lo = sb("w_lo", [P, 4, KT, H], F32R)
        w_gc = sb("w_gc", [P, KT, H])
        wf = sb("wf", [P, 2, H])
        ident = sb("ident", [P, P])
        fc_in = y_out[0:OF, 0]
        attn_in = sb("attn_in", [OF, 2])
        gate_b = sb("gate_b", [P, KT])
        half_b = sb("half_b", [P, KT])
        f12 = sb("f12", [P, 2, 2, NT])
        z_max = sb("z_max", [P, NT])
        z_nmf = sb("z_nmf", [P, NT])
        z_bias = sb("z_bias", [P, NT])
        z_sum = sb("z_sum", [P, NT])
        z_rec = sb("z_rec", [P, NT])
        valid = sb("valid", [P, 2, NT])
        s_min = sb("s_min", [P, U])
        s_sum = sb("s_sum", [P, NH, NT])
        s_val = sb("s_val", [P, NH, NT])
        s_rec = sb("s_rec", [P, NH, NT])
        s_wide = sb("s_wide", [P, NT, HPH, DK])
        stats = sb("stats", [P, 2, NT, 6])
        mean_var = sb("mean_var", [P, 2, NT, 2])
        var_eps = sb("var_eps", [P, 2, NT])
        rstd = sb("rstd", [P, 2, NT])
        neg_mean = sb("neg_mean", [P, 2])
        mean_rstd = sb("mean_rstd", [P, NT])
        neg_half = sb("neg_half", [P, NT])

        ps_s = [ctx.enter_context(nc.psum_tensor(f"ps_s{k}", [P, N], F32)) for k in range(2)]
        ps_t = [ctx.enter_context(nc.psum_tensor(f"ps_t{k}", [P, N], F32)) for k in range(2)]
        ps_c = ctx.enter_context(nc.psum_tensor("ps_c", [P, N], F32))
        misc = [ctx.enter_context(nc.psum_tensor(f"misc{k}", [P, N], F32)) for k in range(3)]

        weights_in = sem("weights_in")
        consts_in = sem("consts_in")
        w_hi_done = sem("w_hi_done")
        w_lo_done = sem("w_lo_done")
        wf_mm = sem("wf_mm")
        wf_done = sem("wf_done")
        half_done = sem("half_done")
        x_loaded = sem("x_loaded")
        adj_loaded = sem("adj_loaded")
        packed = [sem(f"packed{h}") for h in range(NH)]
        stored = sem("stored")
        f_done = sem("f_done")
        mask_a = sem("mask_a")
        mask_b = sem("mask_b")
        f2_rows = sem("f2_rows")
        z_masked = sem("z_masked")
        z_added = sem("z_added")
        z_leaky = sem("z_leaky")
        z_nmf_done = sem("z_nmf_done")
        z_bias_done = sem("z_bias_done")
        z_exp = sem("z_exp")
        z_turned = sem("z_turned")
        z_copied = sem("z_copied")
        z_rec_done = sem("z_rec_done")
        agg_done = sem("agg_done")
        h_done = sem("h_done")
        e_done = sem("e_done")
        res_done = sem("res_done")
        y1_done = sem("y1_done")
        stats1 = sem("stats1")
        aggr1 = sem("aggr1")
        rstd1 = sem("rstd1")
        x1_front = sem("x1_front")
        x1_back = sem("x1_back")
        x1_turned = sem("x1_turned")
        x1_copied = sem("x1_copied")
        x1_hi_done = sem("x1_hi_done")
        x1_lo_done = sem("x1_lo_done")
        qk_mm = sem("qk_mm")
        qk_hi = sem("qk_hi")
        qk_lo = sem("qk_lo")
        v_mm = sem("v_mm")
        v_done = sem("v_done")
        s_mm = sem("s_mm")
        s_masked = sem("s_masked")
        s_exp = sem("s_exp")
        p_turned = sem("p_turned")
        p_scalar = sem("p_scalar")
        p_vector = sem("p_vector")
        c_mm = sem("c_mm")
        sum_valid = sem("sum_valid")
        rec_done = sem("rec_done")
        rec_wide = sem("rec_wide")
        rec_rows = sem("rec_rows")
        rec_copied = sem("rec_copied")
        c_done = sem("c_done")
        gate_mm = sem("gate_mm")
        tanh_done = sem("tanh_done")
        ds_done = sem("ds_done")
        u_done = sem("u_done")
        y2_done = sem("y2_done")
        y_turned = sem("y_turned")
        stats2 = sem("stats2")
        aggr2 = sem("aggr2")
        rstd2 = sem("rstd2")
        applied = sem("applied")

        block = ctx.enter_context(nc.Block())

        def run(eng, step):
            def apart(b):
                step(b, attend=0 <= b < B, pre=b < B - 1, post=1 <= b <= B, late=b >= 2, ahead=b < B - 2)

            for b in range(-1, 3):
                apart(b)
            with eng.Fori(0, (B - 6) // 2) as i:
                for k in range(2):
                    step(2 * i + 3 + k, attend=True, pre=True, post=True, late=True, ahead=True, parity=(3 + k) % 2)
            for b in range(B - 3, B + 2):
                apart(b)

        @block.sync
        def _(sp):
            sp.dma_start(ident[:], eye).then_inc(consts_in, 16)
            sp.dma_start(fc_in, w_fc).then_inc(consts_in, 16)
            sp.dma_start(attn_in[:], w_attn).then_inc(consts_in, 16)
            sp.dma_start(gate_b[:], bg).then_inc(consts_in, 16)

            def load_x(g, par):
                src = x[bass.ds(g, 1)].rearrange("g (t p) i -> p (g t) i", p=P)
                sp.dma_start(x_in[:, par], src).then_inc(x_loaded, 16)

            def load_adj(g):
                src = adj[bass.ds(g, 1)].rearrange("g (t p) m -> p (g t) m", p=P)
                sp.dma_start(adj_in[:], src).then_inc(adj_loaded, 16)

            load_x(0, 0)
            load_adj(0)
            raw = probs_t[:].rearrange("p a h k q -> p (a h k) q")
            for n, w in enumerate((wq_t, wk_t, wv_t)):
                sp.dma_start(raw[:, KT * n:KT * n + KT], w.rearrange("(t p) o -> p t o", p=P)).then_inc(weights_in, 16)
            sp.dma_start(raw[:, 3 * KT:4 * KT], wg_t[H:2 * H].rearrange("(t p) o -> p t o", p=P)).then_inc(weights_in, 16)
            sp.dma_start(w_gc[:], wg_t[0:H].rearrange("(t p) o -> p t o", p=P)).then_inc(weights_in, 16)

            def pack_head(half, j):
                h = half * HPH + j
                rows = slice(j * DK, j * DK + DK)
                for part in range(PARTS):
                    q_lo, k_lo = part // 2, part % 2
                    first, second = 4 * half + q_lo, 4 * half + 2 + k_lo
                    sp.dma_start(qk_pack[part * DK:part * DK + DK, h].bitcast(F32),
                                 stage[rows, first:second + 1:second - first].bitcast(F32)).then_inc(packed[h], 16)

            def step(b, attend, pre, post, late, ahead, parity=None):
                par = b % 2 if parity is None else parity
                if isinstance(b, int) and b == -1:
                    sp.wait_ge(f_done, 2 * NT)
                if ahead:
                    wait(sp, res_done, 2 * b + 2)
                    hold(sp)
                    load_x(b + 2, par)
                if ahead:
                    wait(sp, mask_a, b + 2)
                    wait(sp, mask_b, b + 2)
                    hold(sp)
                    load_adj(b + 2)
                if late:
                    sp.wait_ge(applied, NT * (b - 1))
                    hold(sp)
                    dst = out[bass.ds(b - 2, 1)].rearrange("g (t p) i -> p (g t) i", p=P)
                    sp.dma_start(dst, y_out[:]).then_inc(stored, 16)
                if attend:
                    for j in range(HPH):
                        if j == 0:
                            sp.wait_ge(qk_lo, 4 * b + 4)
                            hold(sp)
                        wait(sp, s_mm, U * (b - 1) + 3 * Q + 2 * j + 2)
                        pack_head(1, j)
                if pre:
                    for j in range(HPH):
                        if j == 0:
                            sp.wait_ge(qk_lo, 4 * (b + 1) + 2)
                            hold(sp)
                        wait(sp, s_mm, U * b + Q + 2 * j + 2)
                        pack_head(0, j)

            run(sp, step)
            sp.wait_ge(stored, 16 * B)

        @block.tensor
        def _(pe):
            mm = nc.tensor.matmul

            pe.wait_ge(consts_in, 64)
            for a in range(2):
                last = mm(misc[0][:, a * H:a * H + H], attn_in[:, a:a + 1].to_broadcast([OF, P]), fc_in,
                          start=True, stop=True)
            last.then_inc(wf_mm, 1)

            def scores(b, u):
                qq, j, r, h, qt = unit(u)
                if qq % 2 == 0 and r == 0:
                    pe.wait_ge(packed[h], PACK * (b + 1))
                wait(pe, s_exp, U * b + u - 1)
                mm(ps_s[u % 2][:], qk_pack[:, h, 0, qt * P:qt * P + P], qk_pack[:, h, 1],
                   start=True, stop=True).then_inc(s_mm, 1)

            def turn(b, u):
                if u >= 2:
                    if by_vector(u - 2):
                        wait(pe, p_vector, NV * b + vector_copies(u - 2))
                    else:
                        wait(pe, p_scalar, (U - NV) * b + scalar_copies(u - 2))
                else:
                    if by_vector(u - 2 + U):
                        wait(pe, p_vector, NV * (b - 1) + vector_copies(u - 2 + U))
                    else:
                        wait(pe, p_scalar, (U - NV) * (b - 1) + scalar_copies(u - 2 + U))
                pe.wait_ge(s_exp, U * b + u + 1)
                for kt in range(NT):
                    last = nc.tensor.transpose(ps_t[u % 2][:, kt * P:kt * P + P],
                                               probs[:, u % 2, kt * P:kt * P + P], ident[:])
                last.then_inc(p_turned, 1)

            def attend_v(b, qq, kt):
                half, qh = qq // 2, qq % 2
                if kt == 0:
                    u = qq * Q + Q - 1
                    pe.wait_ge(p_vector, NV * b + vector_copies(u))
                    pe.wait_ge(p_scalar, (U - NV) * b + scalar_copies(u))
                    if qq == 0:
                        pe.wait_ge(v_done, 2 * b + 2)
                    if qh == 0:
                        wait(pe, c_done, 2 * b + half)
                for j in range(HPH):
                    h = half * HPH + j
                    last = mm(ps_c[j * DK:j * DK + DK, qh * 2 * P:qh * 2 * P + 2 * P], v[:, kt, h * DK:h * DK + DK],
                              probs_t[:, qq % 2, j, kt], start=(kt == 0), stop=(kt == NT - 1))
                if kt == NT - 1:
                    last.then_inc(c_mm, 1)

            def recip_rows(b, half, bank):
                pe.wait_ge(rec_wide, 2 * b + half + 1)
                for qt in range(NT):
                    last = nc.tensor.transpose(bank[:, qt * P:qt * P + P], s_wide[:, qt].rearrange("p j d -> p (j d)"),
                                               ident[:])
                last.then_inc(rec_rows, 1)

            def split_mm(dst, pairs, start=True, stop=True):
                for n, (a, c) in enumerate(pairs):
                    last = mm(dst, a, c, start=start and n == 0, stop=stop and n == len(pairs) - 1)
                return last

            def step(b, attend, pre, post, late, ahead, parity=None):
                par = b % 2 if parity is None else parity
                nxt, prv = 1 - par, 1 - par
                p, q = b + 1, b - 1
                for u in range(U):
                    if attend:
                        scores(b, u)
                    for n in range(4 * NT):
                        if u == PE_V[n] and attend:
                            attend_v(b, n // NT, n % NT)
                        if u == PE_V[n] - U and post:
                            attend_v(q, n // NT, n % NT)

                    if u >= 2 and attend:
                        turn(b, u - 2)
                    if u < 2 and post:
                        turn(q, u - 2 + U)
                    if u == 0 and attend:
                        pe.wait_ge(qk_lo, 4 * b + 4)
                    if u == 0 and pre:
                        if isinstance(p, int) and p == 0:
                            pe.wait_ge(wf_done, 1)
                        pe.wait_ge(f_done, 2 * NT * p + 2 * NT)
                        for t in range(NT):
                            last = nc.tensor.transpose(misc[0][:, t * P:t * P + P],
                                                       f12[:, nxt, 1, t:t + 1].to_broadcast([P, P]), ident[:])
                        last.then_inc(f2_rows, 1)
                    if u == PE_ROWS1 and post:
                        wait(pe, applied, NT * q)
                        recip_rows(q, 1, misc[2])
                    if u in PE_PROJ_V and attend:
                        t = PE_PROJ_V.index(u)
                        if t == 0:
                            wait(pe, applied, NT * q - 2)
                            pe.wait_ge(x1_lo_done, KT * b + KT)
                        if t == 2 and pre:
                            pe.wait_ge(z_masked, NT * p + NT)
                        rows = slice(t * P, t * P + P)
                        pairs = [(a[:, par, kt, rows], w[:, 2, kt]) for kt in range(KT)
                                 for a, w in ((x1_hi, w_hi), (x1_hi, w_lo), (x1_lo, w_hi))]
                        last = split_mm(misc[1 - t // 2][:, t % 2 * H:t % 2 * H + H], pairs)
                        if t % 2 == 1:
                            last.then_inc(v_mm, 1)
                    if u in PE_TURN_Z and pre:
                        t = PE_TURN_Z.index(u)
                        if t == 0 and post:
                            pe.wait_ge(rec_copied, 2 * b)
                        if t == 1 and attend:
                            pe.wait_ge(v_done, 2 * b + 1)
                        if t >= 2:
                            pe.wait_ge(z_copied, NT * p + t - 1)
                        pe.wait_ge(z_exp, NT * p + t + 1)
                        bank = misc[2 - t % 2]
                        for mt in range(NT):
                            last = nc.tensor.transpose(bank[:, mt * P:mt * P + P], z[:, t, mt * P:mt * P + P], ident[:])
                        last.then_inc(z_turned, 1)
                    if u in PE_AGG and pre:
                        t, part = divmod(PE_AGG.index(u), 2)
                        mts = (2 * part, 2 * part + 1)
                        if t == 0 and part == 0 and attend:
                            pe.wait_ge(v_done, 2 * b + 2)
                        if t == 0 and part == 0 and not attend:
                            pe.wait_ge(z_masked, NT * p + NT)
                        if t == 2 and part == 0:
                            pe.wait_ge(z_copied, NT * p + 4)
                        elif part == 0:
                            pe.wait_ge(z_copied, NT * p + t + 1)
                        bank = misc[t // 2]
                        for mt in mts:
                            last = mm(bank[:, t % 2 * H:t % 2 * H + H], z_t[:, mt, t * P:t * P + P], x_in[:, nxt, mt],
                                      start=(mt == 0), stop=(mt == NT - 1))
                        if t % 2 == 1 and part == 1:
                            last.then_inc(agg_done, 1)
                    if u in PE_GATE_X and post:
                        oh = PE_GATE_X.index(u)
                        if oh == 0 and not pre:
                            pe.wait_ge(rec_copied, 2 * b)
                        if oh == 1:
                            if pre:
                                pe.wait_ge(h_done, NT * p + 2)
                            elif attend:
                                pe.wait_ge(v_done, 2 * b + 2)
                        cols = slice(oh * P, oh * P + P)
                        pairs = [(w[:, 3, kt, cols], a[:, prv, kt]) for kt in range(KT)
                                 for w, a in ((w_hi, x1_hi), (w_lo, x1_hi), (w_hi, x1_lo))]
                        split_mm(misc[2 - 2 * oh][:], pairs, stop=False)
                    if u in PE_GATE_C and post:
                        oh = PE_GATE_C.index(u)
                        if oh == 0:
                            pe.wait_ge(c_done, 2 * b)
                        cols = slice(oh * P, oh * P + P)
                        pairs = [(w_gc[:, kt, cols], c_t[:, kt]) for kt in range(KT)]
                        split_mm(misc[2 - 2 * oh][:], pairs, start=False).then_inc(gate_mm, 1)
                    if u == PE_ROWS0 and attend:
                        if post:
                            pe.wait_ge(tanh_done, 2 * q + 1)
                        recip_rows(b, 0, misc[2])
                    if u == PE_TURN_X and pre:
                        for kt in range(KT):
                            if kt == 0:
                                pe.wait_ge(h_done, NT * p + NT)
                                pe.wait_ge(x1_front, 2 * p + 2)
                                pe.wait_ge(x1_back, 2 * p + 2)
                            elif attend:
                                pe.wait_ge(rec_copied, 2 * b + 1)
                            for t in range(NT):
                                last = nc.tensor.transpose(misc[1 + kt][:, t * P:t * P + P],
                                                           hx[:, t, kt * P:kt * P + P], ident[:])
                            last.then_inc(x1_turned, 1)
                    if u in PE_PROJ_QK and pre:
                        n = PE_PROJ_QK.index(u)
                        if n == 0:
                            if isinstance(p, int) and p == 0:
                                pe.wait_ge(w_lo_done, 4)
                            pe.wait_ge(x1_lo_done, KT * p + KT)
                            if post:
                                pe.wait_ge(tanh_done, 2 * q + 2)
                        if n == 3:
                            pe.wait_ge(qk_lo, 4 * p + 1)
                        cols = slice(n // 2 * P, n // 2 * P + P)
                        w0 = n % 2
                        pairs = [(w[:, w0, kt, cols], a[:, nxt, kt]) for kt in range(KT)
                                 for w, a in ((w_hi, x1_hi), (w_lo, x1_hi), (w_hi, x1_lo))]
                        split_mm(misc[n % 3][:], pairs).then_inc(qk_mm, 1)
                    if u in PE_TURN_Y and post:
                        n = PE_TURN_Y.index(u)
                        if n == 0:
                            pe.wait_ge(y2_done, b)
                        if pre:
                            pe.wait_ge(qk_lo, 4 * p + 2 + n)
                        elif n == 0 and attend:
                            pe.wait_ge(v_done, 2 * b + 1)
                        elif n == 1 and attend:
                            pe.wait_ge(rec_copied, 2 * b + 1)
                        elif n == 1:
                            pe.wait_ge(tanh_done, 2 * q + 1)
                        for t in (2 * n, 2 * n + 1):
                            for kt in range(KT):
                                last = nc.tensor.transpose(
                                    misc[1 + n][:, t % 2 * H + kt * P:t % 2 * H + kt * P + P],
                                    summ[:, kt, t * P:t * P + P], ident[:])
                        last.then_inc(y_turned, 1)

            run(pe, step)

        @block.vector
        def _(dve):
            vec = nc.vector
            raw = probs_t[:].rearrange("p a h k q -> p (a h k) q")
            vec.memset(neg_half[:], -0.5).then_inc(half_done, 1)
            dve.wait_ge(consts_in, 64)
            vec.tensor_scalar(half_b[:], gate_b[:], 0.5, None, ALU.mult).then_inc(half_done, 1)
            dve.wait_ge(wf_mm, 1)
            vec.tensor_copy(wf[:], misc[0][:].rearrange("p (a i) -> p a i", a=2)).then_inc(wf_done, 1)
            dve.wait_ge(wf_done, 1)

            def split_weights(n):
                if n == 0:
                    dve.wait_ge(weights_in, 80)
                vec.tensor_copy(w_hi[:, n], raw[:, KT * n:KT * n + KT]).then_inc(w_hi_done, 1)
                dve.wait_ge(w_hi_done, n + 1)
                vec.tensor_tensor(w_lo[:, n], raw[:, KT * n:KT * n + KT], w_hi[:, n].bitcast(F32),
                                  ALU.subtract).then_inc(w_lo_done, 1)

            def node_terms(g, par, t):
                if t == 0:
                    dve.wait_ge(x_loaded, 16 * g + 16)
                for a in range(2):
                    wait(dve, f_done, 2 * NT * g + 2 * t + a - 1)
                    vec.tensor_tensor_reduce(y_out[:, (2 * t + a) % 2], x_in[:, par, t], wf[:, a], 1.0, 0.0,
                                             ALU.mult, ALU.add, f12[:, par, a, t:t + 1]).then_inc(f_done, 1)

            def copy_turned(b, u):
                qq, j, r, h, qt = unit(u)
                dve.wait_ge(p_turned, U * b + u + 1)
                wait(dve, c_mm, 4 * b + qq - 1)
                vec.tensor_copy(probs_t[:, qq % 2, j, :, r * P:r * P + P],
                                ps_t[u % 2][:].rearrange("p (k q) -> p k q", k=NT)).then_inc(p_vector, 1)

            def recip(b, half, par):
                hs = slice(half * HPH, half * HPH + HPH)
                dve.wait_ge(s_exp, U * b + U // 2 * (half + 1))
                vec.tensor_tensor(s_val[:, hs], s_sum[:, hs],
                                  valid[:, par].unsqueeze(1).to_broadcast([P, HPH, NT]), ALU.mult).then_inc(sum_valid, 1)
                dve.wait_ge(sum_valid, 2 * b + half + 1)
                vec.reciprocal(s_rec[:, hs], s_val[:, hs]).then_inc(rec_done, 1)
                dve.wait_ge(rec_done, 2 * b + half + 1)
                wait(dve, rec_rows, 2 * b + half)
                vec.tensor_copy(s_wide[:], s_rec[:, hs].rearrange("p j t -> p t j").unsqueeze(3)
                                .to_broadcast([P, NT, HPH, DK])).then_inc(rec_wide, 1)

            def normalise(b, half):
                dve.wait_ge(c_mm, 4 * b + 2 * half + 2)
                dve.wait_ge(rec_copied, 2 * b + half + 1)
                wait(dve, gate_mm, 2 * b)
                wait(dve, ds_done, 2 * b)
                vec.tensor_tensor(c_t[:, half], ps_c[:], recip_b[:], ALU.mult).then_inc(c_done, 1)

            def step(b, attend, pre, post, late, ahead, parity=None):
                par = b % 2 if parity is None else parity
                nxt, prv = 1 - par, 1 - par
                p, q = b + 1, b - 1
                if isinstance(b, int) and b == -1:
                    for t in range(NT):
                        node_terms(0, 0, t)
                    dve.wait_ge(adj_loaded, 16)
                    vec.tensor_scalar(mask_add[:, 0, 0:2], adj_in[:, 0:2], 0.0, MASKED,
                                      ALU.is_equal, ALU.mult).then_inc(mask_a, 1)
                for u in range(U):
                    if 8 <= u < 12 and isinstance(b, int) and b == -1:
                        split_weights(u - 8)
                    if u >= 3 and by_vector(u - 3) and attend:
                        copy_turned(b, u - 3)
                    if u < 3 and by_vector(u - 3 + U) and post:
                        copy_turned(q, u - 3 + U)
                    if attend:
                        qt = unit(u)[4]
                        dve.wait_ge(s_mm, U * b + u + 1)
                        hold(dve)
                        vec.tensor_tensor_reduce(ps_s[u % 2][:], ps_s[u % 2][:], mask_add[:, par, qt], -SCALE, BIG,
                                                 ALU.add, ALU.min, s_min[:, u:u + 1]).then_inc(s_masked, 1)
                    if u in DVE_MASK_Z and pre:
                        t = DVE_MASK_Z.index(u)
                        if t == 0:
                            wait(dve, z_turned, NT * p)
                            dve.wait_ge(f2_rows, p + 1)
                        dve.wait_ge(mask_b if t >= 2 else mask_a, p + 1)
                        hold(dve)
                        vec.tensor_tensor_reduce(z[:, t], misc[0][:], mask_add[:, nxt, t], 1.0, -BIG,
                                                 ALU.add, ALU.max, z_max[:, t:t + 1]).then_inc(z_masked, 1)
                    if u == DVE_MASK_B and pre:
                        dve.wait_ge(adj_loaded, 16 * p + 16)
                        wait(dve, s_masked, U * b)
                        vec.tensor_scalar(mask_add[:, nxt, 2:4], adj_in[:, 2:4], 0.0, MASKED,
                                          ALU.is_equal, ALU.mult).then_inc(mask_b, 1)
                    if u == DVE_RECIP1 and post:
                        recip(q, 1, prv)
                    if u == DVE_BIAS and pre:
                        dve.wait_ge(z_masked, NT * p + NT)
                        vec.scalar_tensor_tensor(z_nmf[:], z_max[:], -1.0, f12[:, nxt, 0], ALU.mult,
                                                 ALU.subtract).then_inc(z_nmf_done, 1)
                        vec.tensor_scalar(valid[:, nxt], z_max[:], MASKED / 10, None, ALU.is_gt).then_inc(z_nmf_done, 1)
                        dve.wait_ge(z_nmf_done, 2 * p + 2)
                        vec.scalar_tensor_tensor(z_bias[:], z_nmf[:], SLOPE, z_nmf[:], ALU.mult,
                                                 ALU.min).then_inc(z_bias_done, 1)
                    if u in DVE_LEAKY and pre:
                        t = DVE_LEAKY.index(u)
                        dve.wait_ge(z_added, NT * p + t + 1)
                        vec.scalar_tensor_tensor(z[:, t], z[:, t], SLOPE, z[:, t], ALU.mult,
                                                 ALU.max).then_inc(z_leaky, 1)
                    if u == DVE_NORM1 and post:
                        normalise(q, 1)
                    if u in DVE_COPY_V and attend:
                        n = DVE_COPY_V.index(u)
                        if n == 0:
                            wait(dve, c_mm, 4 * b)
                        dve.wait_ge(v_mm, 2 * b + n + 1)
                        vec.tensor_copy(v[:, 2 * n:2 * n + 2],
                                        misc[1 - n][:].rearrange("p (t i) -> p t i", t=2)).then_inc(v_done, 1)
                    if u == DVE_Z_REC and pre:
                        dve.wait_ge(z_exp, NT * p + NT)
                        vec.reciprocal(z_rec[:], z_sum[:]).then_inc(z_rec_done, 1)
                    if u in DVE_NODE and ahead:
                        t = DVE_NODE.index(u)
                        if t == 0:
                            wait(dve, stored, 16 * (b - 1))
                        node_terms(b + 2, par, t)
                    if u in DVE_RES and pre:
                        n = DVE_RES.index(u)
                        pair = slice(2 * n, 2 * n + 2)
                        dve.wait_ge(e_done, 2 * p + n + 1)
                        dve.wait_ge(h_done, NT * p + 2 * n + 2)
                        vec.scalar_tensor_tensor(hx[:, pair], hx[:, pair], 0.0, x_in[:, nxt, pair],
                                                 ALU.max, ALU.add).then_inc(res_done, 1)
                        dve.wait_ge(res_done, 2 * p + n + 1)
                        vec.scalar_tensor_tensor(ey[:, pair], ey[:, pair], 1.0, hx[:, pair],
                                                 ALU.min, ALU.add).then_inc(y1_done, 1)
                    if u in DVE_STATS1 and pre:
                        n = DVE_STATS1.index(u)
                        dve.wait_ge(y1_done, 2 * p + n + 1)
                        for t in (2 * n, 2 * n + 1):
                            vec.bn_stats(stats[:, 0, t], ey[:, t]).then_inc(stats1, 1)
                        wait(dve, (x1_front, x1_back)[n], 2 * p)
                        for t in (2 * n, 2 * n + 1):
                            dve.wait_ge(stats1, NT * p + t + 1)
                            hold(dve)
                            vec.bn_aggr(mean_var[:, 0, t], stats[:, 0, t]).then_inc(aggr1, 1)
                    if u == DVE_RECIP0 and attend:
                        recip(b, 0, par)
                    if u == DVE_GATED and post:
                        dve.wait_ge(tanh_done, 2 * q + 2)
                        dve.wait_ge(ds_done, 2 * q + 2)
                        vec.scalar_tensor_tensor(diff[:], th[:], 3.0, diff[:], ALU.add, ALU.mult).then_inc(u_done, 1)
                    if u == DVE_SPLIT_X and pre:
                        if post:
                            dve.wait_ge(gate_mm, 2 * b)
                        for kt in range(KT):
                            dve.wait_ge(x1_copied, KT * p + kt + 1)
                            vec.tensor_copy(x1_hi[:, nxt, kt], x1_t[:, nxt, kt]).then_inc(x1_hi_done, 1)
                            dve.wait_ge(x1_hi_done, KT * p + kt + 1)
                            vec.tensor_tensor(x1_lo[:, nxt, kt], x1_t[:, nxt, kt], x1_hi[:, nxt, kt].bitcast(F32),
                                              ALU.subtract).then_inc(x1_lo_done, 1)
                    if u == DVE_NORM0 and attend:
                        normalise(b, 0)
                    if u == DVE_X1 and pre:
                        dve.wait_ge(rstd1, 5 * p + 5)
                        for t in (2, 3):
                            vec.tensor_scalar(hx[:, t], ey[:, t], mean_var[:, 0, t, 0:1], rstd[:, 0, t:t + 1],
                                              ALU.subtract, ALU.mult).then_inc(x1_back, 1)
                    if u in DVE_STAGE and pre:
                        n = DVE_STAGE.index(u)
                        dve.wait_ge(qk_hi, 4 * p + n + 1)
                        vec.tensor_tensor(stage[:, 2 * n + 1], misc[n % 3][:], stage[:, 2 * n].bitcast(F32),
                                          ALU.subtract).then_inc(qk_lo, 1)
                    if u in DVE_STATS2 and post:
                        n = DVE_STATS2.index(u)
                        dve.wait_ge(y_turned, 2 * q + n + 1)
                        for t in (2 * n, 2 * n + 1):
                            vec.bn_stats(stats[:, 1, t], misc[1 + n][:, t % 2 * H:t % 2 * H + H]).then_inc(stats2, 1)
                        for t in (2 * n, 2 * n + 1):
                            dve.wait_ge(stats2, NT * q + t + 1)
                            hold(dve)
                            vec.bn_aggr(mean_var[:, 1, t], stats[:, 1, t]).then_inc(aggr2, 1)

            run(dve, step)

        @block.scalar
        def _(act):
            fun = nc.scalar.activation

            def copy_turned(b, u):
                qq, j, r, h, qt = unit(u)
                act.wait_ge(p_turned, U * b + u + 1)
                wait(act, c_mm, 4 * b + qq - 1)
                nc.scalar.copy(probs_t[:, qq % 2, j, :, r * P:r * P + P],
                               ps_t[u % 2][:].rearrange("p (k q) -> p k q", k=NT)).then_inc(p_scalar, 1)

            def copy_recip(b, half, bank):
                act.wait_ge(rec_rows, 2 * b + half + 1)
                wait(act, c_done, 2 * b + half)
                nc.scalar.copy(recip_b[:], bank[:]).then_inc(rec_copied, 1)

            def step(b, attend, pre, post, late, ahead, parity=None):
                par = b % 2 if parity is None else parity
                nxt = 1 - par
                p, q = b + 1, b - 1
                for u in range(U):
                    if u >= 3 and not by_vector(u - 3) and attend:
                        copy_turned(b, u - 3)
                    if u < 3 and not by_vector(u - 3 + U) and post:
                        copy_turned(q, u - 3 + U)
                    if attend:
                        qq, j, r, h, qt = unit(u)
                        wait(act, p_turned, U * b + u - 1)
                        act.wait_ge(s_masked, U * b + u + 1)
                        fun(probs[:, u % 2], ps_s[u % 2][:], ACT.Exp, bias=s_min[:, u:u + 1], scale=-1.0,
                            accum_out=s_sum[:, h, qt:qt + 1]).then_inc(s_exp, 1)
                    if u in ACT_APPLY and late:
                        n = ACT_APPLY.index(u)
                        if n == 0:
                            wait(act, stored, 16 * (b - 2))
                            act.wait_ge(f_done, 2 * NT * (min(b + 1, B) if isinstance(b, int) else b + 1))
                            act.wait_ge(rstd2, 4 * q)
                        for t in (2 * n, 2 * n + 1):
                            fun(y_out[:, t], misc[1 + t // 2][:, t % 2 * H:t % 2 * H + H], ACT.Identity,
                                bias=mean_rstd[:, t:t + 1], scale=rstd[:, 1, t:t + 1]).then_inc(applied, 1)
                    if u == ACT_ROWS1 and post:
                        copy_recip(q, 1, misc[2])
                    if u in ACT_EXP_Z and pre:
                        t = ACT_EXP_Z.index(u)
                        if t == 0:
                            act.wait_ge(z_bias_done, p + 1)
                            wait(act, z_rec_done, p)
                        act.wait_ge(z_leaky, NT * p + t + 1)
                        fun(z[:, t], z[:, t], ACT.Exp, bias=z_bias[:, t:t + 1],
                            accum_out=z_sum[:, t:t + 1]).then_inc(z_exp, 1)
                    if u in ACT_COPY_Z and pre:
                        t = ACT_COPY_Z.index(u)
                        if t == 0:
                            wait(act, agg_done, 2 * p)
                        act.wait_ge(z_turned, NT * p + t + 1)
                        nc.scalar.copy(z_t[:, :, t * P:t * P + P],
                                       misc[2 - t % 2][:].rearrange("p (m n) -> p m n", m=NT)).then_inc(z_copied, 1)
                    if u in ACT_AGG and pre:
                        n = ACT_AGG.index(u)
                        pair = slice(2 * n, 2 * n + 2)
                        act.wait_ge(agg_done, 2 * p + n + 1)
                        act.wait_ge(z_rec_done, p + 1)
                        wait(act, x1_turned, KT * p)
                        for t in (2 * n, 2 * n + 1):
                            fun(hx[:, t], misc[n][:, t % 2 * H:t % 2 * H + H], ACT.Identity,
                                scale=z_rec[:, t:t + 1]).then_inc(h_done, 1)
                        act.wait_ge(h_done, NT * p + 2 * n + 2)
                        wait(act, (x1_front, x1_back)[n], 2 * p)
                        fun(ey[:, pair], hx[:, pair], ACT.Exp).then_inc(e_done, 1)
                    if u in ACT_TANH and post:
                        oh = ACT_TANH.index(u)
                        act.wait_ge(gate_mm, 2 * q + oh + 1)
                        wait(act, u_done, q)
                        fun(th[:, oh], misc[2 - 2 * oh][:], ACT.Tanh, bias=half_b[:, oh:oh + 1],
                            scale=0.5).then_inc(tanh_done, 1)
                    if u == ACT_ROWS0 and attend:
                        copy_recip(b, 0, misc[2])
                    if u == ACT_COPY_X and pre:
                        for kt in range(KT):
                            act.wait_ge(x1_turned, KT * p + kt + 1)
                            if post:
                                act.wait_ge(ds_done, 2 * b)
                            nc.scalar.copy(x1_t[:, nxt, kt], misc[1 + kt][:]).then_inc(x1_copied, 1)
                    if u in ACT_STAGE and pre:
                        n = ACT_STAGE.index(u)
                        act.wait_ge(qk_mm, 4 * p + n + 1)
                        wait(act, s_mm, U * b + (Q if n < 2 else 3 * Q))
                        nc.scalar.copy(stage[:, 2 * n], misc[n % 3][:]).then_inc(qk_hi, 1)

            act.wait_ge(half_done, 2)
            run(act, step)

        @block.gpsimd
        def _(pool):
            gp = nc.gpsimd

            def inverse_std(which, tiles, eps, done, base):
                gp.tensor_scalar(var_eps[:, which, tiles], mean_var[:, which, tiles, 1], eps, 1.0, ALU.add,
                                 ALU.mult).then_inc(done, 1)
                pool.wait_ge(done, base + 1)
                gp.tensor_tensor(rstd[:, which, tiles], var_eps[:, which, tiles], neg_half[:, tiles],
                                 ALU.pow).then_inc(done, 1)

            def mask_front(g, par):
                pool.wait_ge(adj_loaded, 16 * g + 16)
                wait(pool, s_masked, U * (g - 2) + 3 * Q)
                wait(pool, z_masked, NT * (g - 2) + NT)
                hold(pool)
                gp.tensor_scalar(mask_add[:, par, 0:2], adj_in[:, 0:2], 0.0, MASKED,
                                 ALU.is_equal, ALU.mult).then_inc(mask_a, 1)

            pool.wait_ge(half_done, 2)

            def step(b, attend, pre, post, late, ahead, parity=None):
                par = b % 2 if parity is None else parity
                nxt, prv = 1 - par, 1 - par
                p, q = b + 1, b - 1
                if pre:
                    for t in range(NT):
                        pool.wait_ge(z_masked, NT * p + t + 1)
                        hold(pool)
                        gp.tensor_scalar(z[:, t], z[:, t], f12[:, nxt, 0, t:t + 1], 1.0, ALU.add,
                                         ALU.mult).then_inc(z_added, 1)
                if post:
                    pool.wait_ge(c_done, 2 * b)
                    wait(pool, y2_done, q)
                    wait(pool, y_turned, 2 * q)
                    gp.tensor_tensor(diff[:], x1_t[:, prv], c_t[:], ALU.subtract).then_inc(ds_done, 1)
                    gp.tensor_scalar(summ[:], c_t[:], 4.0, 0.0, ALU.mult, ALU.add).then_inc(ds_done, 1)
                if pre:
                    pool.wait_ge(aggr1, NT * p + 2)
                    hold(pool)
                    gp.tensor_scalar(neg_mean[:], mean_var[:, 0, 0:2, 0], -1.0, 0.0, ALU.mult, ALU.add).then_inc(rstd1, 1)
                    inverse_std(0, slice(0, 2), EPS, rstd1, 5 * p + 1)
                    pool.wait_ge(rstd1, 5 * p + 3)
                    hold(pool)
                    for t in (0, 1):
                        gp.tensor_scalar(hx[:, t], ey[:, t], neg_mean[:, t:t + 1], rstd[:, 0, t:t + 1], ALU.add,
                                         ALU.mult).then_inc(x1_front, 1)
                    pool.wait_ge(aggr1, NT * p + NT)
                    hold(pool)
                    inverse_std(0, slice(2, NT), EPS, rstd1, 5 * p + 3)
                if ahead:
                    mask_front(b + 2, par)
                if post:
                    pool.wait_ge(u_done, b)
                    gp.tensor_tensor(summ[:], summ[:], diff[:], ALU.add).then_inc(y2_done, 1)
                if post:
                    pool.wait_ge(aggr2, NT * b)
                    hold(pool)
                    inverse_std(1, slice(0, NT), 4 * EPS, rstd2, 4 * q)
                    wait(pool, applied, NT * q)
                    hold(pool)
                    gp.tensor_scalar(mean_rstd[:], mean_var[:, 1, :, 0], -1.0, 0.0, ALU.mult, ALU.add).then_inc(rstd2, 1)
                    pool.wait_ge(rstd2, 4 * q + 3)
                    gp.tensor_tensor(mean_rstd[:], mean_rstd[:], rstd[:, 1], ALU.mult).then_inc(rstd2, 1)

            run(pool, step)


def kernel(**inputs):
    import numpy as _np
    import concourse.bacc as _bacc
    from concourse.bass_utils import run_bass_kernel_spmd as _run

    given = {
        "x": inputs["x"],
        "adj": inputs["adj"],
        "w_fc": inputs["L0_gnn_W_fc"],
        "w_attn": _np.asarray(inputs["L0_gnn_W_attn"]).reshape(2, -1).T,
        "wq_t": _np.asarray(inputs["L1_gnn_Wq"]).T,
        "wk_t": _np.asarray(inputs["L1_gnn_Wk"]).T,
        "wv_t": _np.asarray(inputs["L1_gnn_Wv"]).T,
        "wg_t": _np.asarray(inputs["L1_gnn_Wg"]).T,
        "bg": _np.asarray(inputs["L1_gnn_bg"]).reshape(-1, P).T,
        "eye": _np.eye(P, dtype=_np.float32),
    }
    nc = _bacc.Bacc("TRN2", target_bir_lowering=False, num_devices=1)
    arrays, args = {}, []
    for name, a in given.items():
        a = _np.ascontiguousarray(a)
        arrays[name] = a
        args.append(nc.dram_tensor(name, a.shape, mybir.dt.from_np(a.dtype), kind="ExternalInput").ap())
    shape = given["x"].shape
    args.append(nc.dram_tensor("out", shape, F32, kind="ExternalOutput").ap())
    two_layer_gat(nc, *args)
    r = _run(nc, [arrays], core_ids=[0])
    return r.results[0]["out"]
```
